# Optimizing a Trainium2 kernel written in Bass

```python
import numpy as np
import jax
import jax.numpy as jnp

def _softmax(x, axis=-1):
    return jax.nn.softmax(x, axis=axis)

def _gelu(x):
    return jax.nn.gelu(x, approximate=True)

def _silu(x):
    return jax.nn.silu(x)

def _sigmoid(x):
    return jax.nn.sigmoid(x)

def _layernorm(x, axis=-1, eps=1e-05):
    m = jnp.mean(x, axis=axis, keepdims=True)
    v = jnp.var(x, axis=axis, keepdims=True)
    return (x - m) / jnp.sqrt(v + eps)

def _scatter_add(tgt, idx, src, axis=0):
    return tgt.at[idx].add(src)

def _segment_sum(src, seg, n):
    return jax.ops.segment_sum(src, seg, n)
kernel_name = 'mk_gnn_resnorm_d2_gnn_r32_7a3b46'

def setup_inputs(seed: int=0):
    np.random.seed(seed)
    _w = jnp.asarray

    def _rec_inputs():
        import jax
        import jax.numpy as jnp
        _gk = jax.random.key(seed)
        x = -0.0006008 + 1.001 * jax.random.normal(jax.random.fold_in(_gk, 1), (50000, 256), jnp.float32)
        src = jax.random.randint(jax.random.fold_in(_gk, 2), (25000,), 0, 50000, jnp.int32)
        dst = jnp.minimum((50000 * jax.random.uniform(jax.random.fold_in(_gk, 3), (25000,)) ** 2.0).astype(jnp.int32), 49999)
        _o = jnp.argsort(dst, stable=True)
        src = src[_o]
        dst = dst[_o]
        edge_attr_256 = -4.21973e-05 + 0.999841 * jax.random.normal(jax.random.fold_in(_gk, 12), (25000, 256), jnp.float32)
        return (x, src, dst, edge_attr_256)
    x, src, dst, edge_attr_256 = _rec_inputs()

    def _L0_gnn_setup():
        import jax, jax.numpy as jnp
        import numpy as np
        N, E, D, L = (10000, 9375, 256, 4)
        BN_EPS = 1e-05

        def _gine_conv(x, e, src, dst, W, b):
            m = jax.nn.relu(x[src] + e)
            aggr = jax.ops.segment_sum(m, dst, num_segments=x.shape[0])
            return jax.nn.relu((x + aggr) @ W + b)

        def _batch_norm(x, g, b):
            mu = x.mean(axis=0)
            var = x.var(axis=0)
            return (x - mu) * jax.lax.rsqrt(var + BN_EPS) * g + b
        key = jax.random.key(seed)
        ks = jax.random.split(key, 8)
        s = 0.05
        return {'node_feat': jax.random.normal(ks[0], (N, D), jnp.float32), 'edge_feat': jax.random.normal(ks[1], (E, D), jnp.float32), 'src': jax.random.randint(ks[2], (E,), 0, N, dtype=jnp.int32), 'dst': jax.random.randint(ks[3], (E,), 0, N, dtype=jnp.int32), 'W_conv': jax.random.normal(ks[4], (L, D, D), jnp.float32) * s, 'b_conv': jnp.zeros((L, D), jnp.float32), 'W_edge': jax.random.normal(ks[5], (L, D, D), jnp.float32) * s, 'b_edge': jnp.zeros((L, D), jnp.float32), 'gamma': jnp.ones((L, D), jnp.float32), 'beta': jnp.zeros((L, D), jnp.float32)}
    _L0_gnn_all = _L0_gnn_setup()
    _L0_gnn_in = {k: v for k, v in _L0_gnn_all.items() if k in ('W_conv', 'b_conv', 'W_edge', 'b_edge', 'gamma', 'beta')}
    del _L0_gnn_all

    def _L1_gnn_setup():
        import jax, jax.numpy as jnp
        import numpy as np
        N_NODES = 10000
        N_EDGES = 10000
        D = 256
        key = jax.random.key(seed)
        k_x, k_w, k_m, k_s, k_d = jax.random.split(key, 5)
        x = jax.random.normal(k_x, (N_NODES, D), dtype=jnp.float32)
        W = jax.random.normal(k_w, (D, D), dtype=jnp.float32)
        M = jax.random.normal(k_m, (D, D), dtype=jnp.float32)
        edge_src = jax.random.randint(k_s, (N_EDGES,), 0, N_NODES, dtype=jnp.int64)
        edge_dst = jax.random.randint(k_d, (N_EDGES,), 0, N_NODES, dtype=jnp.int64)
        return {'x': x, 'W': W, 'M': M, 'edge_src': edge_src, 'edge_dst': edge_dst}
    _L1_gnn_all = _L1_gnn_setup()
    _L1_gnn_in = {k: v for k, v in _L1_gnn_all.items() if k in ('W', 'M')}
    del _L1_gnn_all
    return {'x': x, 'src': src, 'dst': dst, 'edge_attr_256': edge_attr_256, 'L0_gnn_W_conv': _L0_gnn_in['W_conv'], 'L0_gnn_b_conv': _L0_gnn_in['b_conv'], 'L0_gnn_W_edge': _L0_gnn_in['W_edge'], 'L0_gnn_b_edge': _L0_gnn_in['b_edge'], 'L0_gnn_gamma': _L0_gnn_in['gamma'], 'L0_gnn_beta': _L0_gnn_in['beta'], 'L1_gnn_W': _L1_gnn_in['W'], 'L1_gnn_M': _L1_gnn_in['M']}

def reference(x, src, dst, edge_attr_256, L0_gnn_W_conv, L0_gnn_b_conv, L0_gnn_W_edge, L0_gnn_b_edge, L0_gnn_gamma, L0_gnn_beta, L1_gnn_W, L1_gnn_M):
    import jax
    import jax.numpy as jnp

    def _L0_gnn_ref(node_feat, edge_feat, src, dst, W_conv, b_conv, W_edge, b_edge, gamma, beta):
        import jax, jax.numpy as jnp
        import numpy as np
        N, E, D, L = (10000, 9375, 256, 4)
        BN_EPS = 1e-05

        def _gine_conv(x, e, src, dst, W, b):
            m = jax.nn.relu(x[src] + e)
            aggr = jax.ops.segment_sum(m, dst, num_segments=x.shape[0])
            return jax.nn.relu((x + aggr) @ W + b)

        def _batch_norm(x, g, b):
            mu = x.mean(axis=0)
            var = x.var(axis=0)
            return (x - mu) * jax.lax.rsqrt(var + BN_EPS) * g + b
        init = node_feat
        x, e = (node_feat, edge_feat)
        for i in range(L):
            x = _gine_conv(x, e, src, dst, W_conv[i], b_conv[i])
            e = jax.nn.relu(e @ W_edge[i] + b_edge[i])
            x = _batch_norm(x, gamma[i], beta[i])
        x = _gine_conv(x, e, src, dst, W_conv[L - 1], b_conv[L - 1])
        return x + init

    def _L1_gnn_ref(x, W, M, edge_src, edge_dst):
        import jax, jax.numpy as jnp
        import numpy as np
        N_NODES = 10000
        N_EDGES = 10000
        D = 256
        self_term = x @ W
        msg = x @ M
        agg = jax.ops.segment_sum(msg[edge_src], edge_dst, num_segments=x.shape[0])
        return jax.nn.relu(self_term + agg)
    x = _layernorm(x + _L0_gnn_ref(x, edge_attr_256, src, dst, L0_gnn_W_conv, L0_gnn_b_conv, L0_gnn_W_edge, L0_gnn_b_edge, L0_gnn_gamma, L0_gnn_beta), axis=-1)
    x = _layernorm(x + _L1_gnn_ref(x, L1_gnn_W, L1_gnn_M, src, dst), axis=-1)
    return x

_drawn_inputs = setup_inputs


def setup_inputs(seed=0):
    import zlib

    import numpy as np

    out = dict(_drawn_inputs(seed))
    spreads = {'L0_gnn_b_conv': (0.0, 0.1),
     'L0_gnn_b_edge': (0.0, 0.402),
     'L0_gnn_gamma': (1.0, 0.2),
     'L0_gnn_beta': (0.0, 0.1)}
    factors = {}
    for name, (base, spread) in spreads.items():
        noise = np.random.default_rng([zlib.crc32(name.encode()), seed]).standard_normal(out[name].shape)
        drawn = base * np.exp(spread * noise) if base else spread * noise
        out[name] = jnp.asarray(drawn.astype(out[name].dtype))
    for name, factor in factors.items():
        out[name] = (out[name] * factor).astype(out[name].dtype)
    return out
```

```python
from contextlib import ExitStack

import concourse.bass as bass
from concourse import mybir

ALU = mybir.AluOpType
ACT = mybir.ActivationFunctionType
F32 = mybir.dt.float32
I32 = mybir.dt.int32

P = 128
D = 256
H = D // P
QUAD = 4
N = 50000
E = 25000
LAYERS = 4
EPS = 1e-5

CHUNKS = -(-E // P)
EP = CHUNKS * P
EGROUPS = CHUNKS // QUAD
CH = CHUNKS // 2
NGROUPS = -(-N // (P * QUAD))
TILES = NGROUPS * QUAD
NP = TILES * P
FULL = (N - (P - 1) * TILES) // QUAD
PAD_DST = 1 << 20
END_DST = 1 << 21
SPAN = EP
ZERO = SPAN + CHUNKS
SUMS = ZERO + P
assert CHUNKS % QUAD == 0 and (N - (P - 1) * TILES) % QUAD == 0


def over_groups(eng, first, last, step):
    g = first
    while g < last and (g < 2 or g % 2):
        step(g // 2, g % 2)
        g += 1
    pairs = (last - g) // 2
    if pairs:
        with eng.Fori(g // 2, g // 2 + pairs) as k:
            step(k, 0)
            step(k, 1)
    g += 2 * pairs
    if g < last:
        step(g // 2, g % 2)


def before(k, p):
    return (k - 1, 1) if p == 0 else (k, 0)


def after(k, p):
    return (k, 1) if p == 0 else (k + 1, 0)


def wait(eng, sem, value):
    if not isinstance(value, int) or value > 0:
        eng.wait_ge(sem, value)


def wait_alone(eng, sem, value, passed):
    wait(eng, sem, value)
    if not isinstance(value, int):
        eng.sem_inc(passed, 1)


def gnn_kernel(nc, x, src, dst, edge, w_conv, b_conv, w_edge, b_edge, gamma, beta, l1_w, l1_m, out):
    ctx = ExitStack()
    with ctx:
        def sb(name, shape, dt=F32):
            return ctx.enter_context(nc.sbuf_tensor(name, shape, dt))

        def sem(name):
            return ctx.enter_context(nc.semaphore(name))

        def slots(name):
            return [sem(f"{name}{i}") for i in range(2)]

        nodes = nc.dram_tensor("nodes", [NP, D], F32).ap()
        sums = nc.dram_tensor("sums", [SUMS, D], F32).ap()
        edge_t = nc.dram_tensor("edge_t", [EGROUPS, P, H * QUAD * P], F32).ap()
        row_of = nc.dram_tensor("row_of", [NP, 1], I32).ap()

        def tiles(ap):
            return ap.rearrange("(p t) f -> p t f", p=P)

        nodes_v, x_v, out_v = tiles(nodes), tiles(x), tiles(out)
        row_of_v = row_of.rearrange("(p t) o -> p (t o)", p=P)
        sums_v = sums[0:EP, :].rearrange("(c p) f -> p c f", p=P)
        edge_v = edge.rearrange("(c p) f -> p c f", p=P)
        dst_groups = dst[0:EP].rearrange("(g j) -> g j", j=QUAD * P)

        def chunk_rows(ap):
            return ap.rearrange("(h q p) -> q h p", h=2, q=CH)

        wc = sb("wc", [P, LAYERS, H, D])
        we = sb("we", [P, LAYERS, H, D])
        w1 = sb("w1", [P, H, D])
        m1 = sb("m1", [P, H, D])
        bc = sb("bc", [P, LAYERS, H])
        be = sb("be", [P, LAYERS, H])
        gam = sb("gam", [P, LAYERS, H])
        bet = sb("bet", [P, LAYERS, H])
        ones = sb("ones", [P, P])
        ident = sb("ident", [P, P])
        sel_last = sb("sel_last", [P, P])
        sel_first = sb("sel_first", [P, P])

        raw = sb("raw", [CH, 3, 2, P], I32)
        rawf = sb("rawf", [CH, 3, 2, P])
        dcol = sb("dcol", [P, CHUNKS])
        dnext = sb("dnext", [P, CHUNKS])
        src_i = sb("src_i", [P, CHUNKS], I32)
        prev_last = sb("prev_last", [P, CHUNKS])
        first_row = sb("first_row", [CH, CHUNKS])
        links = sb("links", [CH, 2, CHUNKS])
        j_i = sb("j_i", [P, CHUNKS], I32)
        span_i = sb("span_i", [P, CHUNKS], I32)
        j_f = sb("j_f", [P, CHUNKS])
        span_f = sb("span_f", [P, CHUNKS])
        flag = sb("flag", [P, CHUNKS])
        row_i = sb("row_i", [P, CHUNKS], I32)
        node_i = sb("node_i", [P, CHUNKS], I32)
        zero_rows = sb("zero_rows", [P, TILES], I32)
        row_stage = sb("row_stage", [P, 2, QUAD], I32)
        node_stage = sb("node_stage", [P, 2, QUAD], I32)

        stats = sb("stats", [P, H, NGROUPS, 6])
        mv = sb("mv", [P, H, 2])
        rstd = sb("rstd", [P, H])
        scale = sb("scale", [P, H])
        shift = sb("shift", [P, H])
        tmp = sb("tmp", [P, H])
        diag = sb("diag", [P, H, P])
        scale_row = sb("scale_row", [P, D])

        idx = sb("idx", [P, 2, QUAD], I32)
        row_idx = sb("row_idx", [P, TILES], I32)
        got = sb("got", [P, 2, QUAD, D])
        ein = sb("ein", [P, 2, QUAD * D])
        rows = sb("rows", [P, 2, QUAD, D])
        tin = sb("tin", [P, 2, H, QUAD * P])
        tout = sb("tout", [P, 2, H, QUAD * P])
        mid = sb("mid", [P, 2, QUAD, D])
        res = sb("res", [P, 2, QUAD, D])
        drow = sb("drow", [P, 2, QUAD * P], I32)
        same = sb("same", [P, 2, QUAD, P])
        ln_stats = sb("ln_stats", [P, 2, QUAD, 6])
        ln_mv = sb("ln_mv", [P, 2, QUAD, 2])
        ln_std = sb("ln_std", [P, 2, QUAD])
        eps = sb("eps", [P, 1])
        bn_std = sb("bn_std", [P, H])
        ln_rstd = sb("ln_rstd", [P, 2, QUAD])
        run_last = sb("run_last", [CH, 2, D])
        run_first = sb("run_first", [CH, 2, D])
        run_sum = sb("run_sum", [CH, 2, D])

        def bank2(name):
            return ctx.enter_context(nc.psum_tensor(name, [P, H, QUAD * P], F32))

        ps_in, ps_agg, ps_out, ps_back = (bank2(n) for n in ("ps_in", "ps_agg", "ps_out", "ps_back"))

        def as_rows(ps):
            return ps[:, :, :].rearrange("p h (k f) -> p (h k) f", f=D)

        loaded = sem("loaded")
        raw_loaded = sem("raw_loaded")
        const_made = sem("const_made")
        prep = sem("prep")
        prep_pe = sem("prep_pe")
        links_made = sem("links_made")
        tables_stored = sem("tables_stored")
        stage_copied = sem("stage_copied")
        row_idx_loaded = sem("row_idx_loaded")
        idx_staged = sem("idx_staged")
        rows_scattered = slots("rows_scattered")

        sp_got, e_loaded, drow_loaded = map(slots, ("sp_got", "e_loaded", "drow_loaded"))
        e_shifted = sem("e_shifted")
        same_made = sem("same_made")
        got_scaled = sem("got_scaled")
        msg_summed = sem("msg_summed")
        msg_made = sem("msg_made")
        e_turned = sem("e_turned")
        e_turned_out = sem("e_turned_out")
        e_product = sem("e_product")
        e_updated = sem("e_updated")
        sums_made = sem("sums_made")
        sums_out = sem("sums_out")
        sums_stored, e_stored = map(slots, ("sums_stored", "e_stored"))
        seg_turned = sem("seg_turned")
        seg_turned_out = sem("seg_turned_out")
        runs_loaded = sem("runs_loaded")
        runs_product = sem("runs_product")
        runs_summed = sem("runs_summed")
        runs_stored = sem("runs_stored")

        rows_loaded, dn_got, nodes_stored, x_loaded = map(
            slots, ("rows_loaded", "dn_got", "nodes_stored", "x_loaded"))
        turned = sem("turned")
        scaled = sem("scaled")
        added = sem("added")
        product = sem("product")
        activated = sem("activated")
        counted = sem("counted")
        back = sem("back")
        rows_out = sem("rows_out")
        ln = sem("ln")
        bn = sem("bn")
        bn_row = sem("bn_row")
        bn_row_out = sem("bn_row_out")
        ln_rstd_made = sem("ln_rstd_made")
        ln_std_made = sem("ln_std_made")
        ln_out = sem("ln_out")
        sp_passed, pool_passed, dve_passed = sem("sp_passed"), sem("pool_passed"), sem("dve_passed")
        bn_std_made = sem("bn_std_made")
        steps = sem("row_steps")

        NS = (EGROUPS + 1) // 2, EGROUPS // 2
        ND = NGROUPS // 2
        SPARSE = LAYERS + 2
        LAST = LAYERS
        FINAL = LAYERS + 1

        BN_STEPS = 6
        LN_STEPS = 4

        def ln_read(d, k, p, ago=0):
            return LN_STEPS * (NGROUPS * (d - LAST) + 2 * k + p - ago) + 2

        block = ctx.enter_context(nc.Block())

        @block.sync
        def _(sp):
            sp.dma_start(raw[:, 0, :, :], chunk_rows(dst[0:EP])).then_inc(raw_loaded, 16)
            sp.dma_start(raw[:, 1, :, :], chunk_rows(dst[1:EP + 1])).then_inc(raw_loaded, 16)
            sp.dma_start(raw[:, 2, :, :], chunk_rows(src)).then_inc(raw_loaded, 16)
            sp.dma_start(wc[:, :, :, :], w_conv).then_inc(loaded, 16)
            sp.dma_start(we[:, :, :, :], w_edge).then_inc(loaded, 16)
            sp.dma_start(w1[:, :, :], l1_w).then_inc(loaded, 16)
            sp.dma_start(m1[:, :, :], l1_m).then_inc(loaded, 16)
            for to, of in ((bc, b_conv), (be, b_edge), (gam, gamma), (bet, beta)):
                sp.dma_start(to[:, :, :], of).then_inc(loaded, 16)
            sp.wait_ge(const_made, 4)
            sp.dma_start(row_of_v, zero_rows[:, :]).then_inc(tables_stored, 16)
            sp.dma_start(sums[ZERO:ZERO + P, :], res[:, 0, 0, :]).then_inc(tables_stored, 16)
            sp.wait_ge(tables_stored, 32)

            def sparse_load(s, k, p):
                g, u = 2 * k + p, NS[p] * s + k
                wait_alone(sp, same_made, EGROUPS * s + g - 1, sp_passed)
                sp.dma_start(drow[:, p, :], dst_groups[bass.ds(g, 1), :].to_broadcast([P, QUAD * P])).then_inc(
                    drow_loaded[p], 16)
                if s == 0:
                    if not isinstance(g, int) or g >= 2:
                        wait_alone(sp, e_turned, g - 1, sp_passed)
                        wait_alone(sp, msg_summed, g - 1, sp_passed)
                    sp.dma_start(ein[:, p, :].rearrange("p (c f) -> p c f", f=D),
                                 edge_v[:, bass.ds(g * QUAD, QUAD), :]).then_inc(e_loaded[p], 16)
                elif s < FINAL:
                    wait_alone(sp, e_shifted, EGROUPS * (s - 1) + g - 1, sp_passed)
                    if s <= LAYERS - 1:
                        wait_alone(sp, e_product, H * (EGROUPS * s + g - 1), sp_passed)
                    sp.dma_start(ein[:, p, :],
                                 edge_t[bass.ds(g, 1), :, :].rearrange("o p f -> (o p) f")).then_inc(e_loaded[p], 16)

            def sparse_store(s, k, p):
                g = 2 * k + p
                wait_alone(sp, sums_out, EGROUPS * s + g + 1, sp_passed)
                sp.dma_start(sums_v[:, bass.ds(g * QUAD, QUAD), :], res[:, p, :, :]).then_inc(sums_stored[p], 16)
                if s < LAYERS:
                    wait_alone(sp, e_updated, H * (EGROUPS * s + g + 1), sp_passed)
                    sp.dma_start(edge_t[bass.ds(g, 1), :, :].rearrange("o p f -> (o p) f"),
                                 tout[:, p, :, :].rearrange("p h j -> p (h j)")).then_inc(e_stored[p], 16)

            def dense_load(d, k, p):
                g, u = 2 * k + p, ND * d + k
                wait_alone(sp, turned, NGROUPS * d + g - 1, sp_passed)
                if d == FINAL:
                    wait_alone(sp, ln, ln_read(d, k, p, 2), sp_passed)
                table = x_v if d == 0 else nodes_v
                sp.dma_start(rows[:, p, :, :], table[:, bass.ds(g * QUAD, QUAD), :]).then_inc(rows_loaded[p], 16)
                if d == LAST:
                    if not isinstance(g, int) or g >= 2:
                        wait_alone(sp, ln, ln_read(d, k, p, 2), sp_passed)
                    sp.dma_start(ein[:, p, :].rearrange("p (t f) -> p t f", f=D),
                                 x_v[:, bass.ds(g * QUAD, QUAD), :]).then_inc(x_loaded[p], 16)

            def dense_store(d, k, p):
                g = 2 * k + p
                if d < LAST:
                    wait_alone(sp, rows_out, NGROUPS * d + g + 1, sp_passed)
                else:
                    wait_alone(sp, ln_out, NGROUPS * (d - LAST) + g + 1, sp_passed)
                table = out_v if d == FINAL else nodes_v
                sp.dma_start(table[:, bass.ds(g * QUAD, QUAD), :], res[:, p, :, :]).then_inc(nodes_stored[p], 16)

            for s in range(SPARSE):
                if s > 0:
                    if s <= LAYERS:
                        for p in range(2):
                            sp.wait_ge(e_stored[p], 16 * NS[p] * s)
                sparse_load(s, 0, 0)

                def sparse_step(k, p):
                    sparse_load(s, *after(k, p))
                    if not (isinstance(k, int) and k == 0 and p == 0):
                        sparse_store(s, *before(k, p))

                over_groups(sp, 0, EGROUPS - 1, sparse_step)
                sparse_store(s, (EGROUPS - 2) // 2, (EGROUPS - 2) % 2)
                sparse_store(s, (EGROUPS - 1) // 2, (EGROUPS - 1) % 2)
                for p in range(2):
                    sp.wait_ge(sums_stored[p], 16 * NS[p] * (s + 1))
                edges = sums[0:EP, :].rearrange("(h q p) f -> q h p f", h=2, q=CH)
                sp.dma_start(run_last[:, :, :], edges[:, :, P - 1, :]).then_inc(runs_loaded, 16)
                sp.dma_start(run_first[:, :, :], edges[:, :, 0, :]).then_inc(runs_loaded, 16)
                if s > 0:
                    for p in range(2):
                        sp.wait_ge(nodes_stored[p], 16 * ND * s)
                else:
                    for p in range(2):
                        sp.wait_ge(rows_scattered[p], 16 * QUAD * NS[p])
                    sp.dma_start(row_idx[:, :], row_of_v).then_inc(row_idx_loaded, 16)
                dense_load(s, 0, 0)
                sp.wait_ge(runs_summed, s + 1)
                sp.dma_start(sums[SPAN:SPAN + CHUNKS, :].rearrange("(h q) f -> q h f", h=2),
                             run_sum[:, :, :]).then_inc(runs_stored, 16)

                def dense_step(k, p):
                    dense_load(s, *after(k, p))
                    if not (isinstance(k, int) and k == 0):
                        dense_store(s, k - 1, p)

                over_groups(sp, 0, NGROUPS - 1, dense_step)
                for g in range(NGROUPS - 3, NGROUPS):
                    dense_store(s, g // 2, g % 2)
                for p in range(2):
                    sp.wait_ge(nodes_stored[p], 16 * ND * (s + 1))

        @block.gpsimd
        def _(pool):
            nc.gpsimd.memset(ones[:, :], 1.0).then_inc(const_made, 1)
            nc.gpsimd.memset(res[:, 0, :, :], 0.0).then_inc(const_made, 1)
            nc.gpsimd.iota(zero_rows[:, :], pattern=[[0, TILES]], base=ZERO, channel_multiplier=1).then_inc(const_made, 1)
            nc.gpsimd.iota(j_i[:, :], pattern=[[P, CHUNKS]], base=0, channel_multiplier=1).then_inc(const_made, 1)
            nc.gpsimd.iota(span_i[:, :], pattern=[[1, CHUNKS]], base=SPAN, channel_multiplier=0).then_inc(const_made, 1)
            pool.wait_ge(const_made, 5)
            nc.gpsimd.affine_select(out=ident[:, :], in_=ones[:, :], compare_op=ALU.is_equal, fill=0.0, base=0,
                                    pattern=[[-1, P]], channel_multiplier=1).then_inc(const_made, 1)
            nc.gpsimd.affine_select(out=sel_last[:, :], in_=ones[:, :], compare_op=ALU.is_equal, fill=0.0,
                                    base=-(P - 1), pattern=[[0, P]], channel_multiplier=1).then_inc(const_made, 1)
            nc.gpsimd.affine_select(out=sel_first[:, :], in_=ones[:, :], compare_op=ALU.is_equal, fill=0.0,
                                    base=0, pattern=[[0, P]], channel_multiplier=1).then_inc(const_made, 1)
            pool.wait_ge(prep, 10)
            for h in range(2):
                nc.gpsimd.affine_select(out=links[:, h, :], in_=links[:, h, :], compare_op=ALU.is_gt, fill=0.0,
                                        base=-CH * h, pattern=[[1, CHUNKS]], channel_multiplier=-1).then_inc(links_made, 1)

            def gather(table, index, to, done):
                nc.gpsimd.indirect_dma_start(
                    out=to, out_offset=None, in_=table,
                    in_offset=bass.IndirectOffsetOnAxis(ap=index, axis=0)).then_inc(done, 16)

            for s in range(SPARSE):
                def sparse_gather(k, p):
                    g, u = 2 * k + p, NS[p] * s + k
                    wait_alone(pool, sp_got[p], 16 * QUAD * u, pool_passed)
                    nc.gpsimd.tensor_copy(idx[:, p, :], src_i[:, bass.ds(g * QUAD, QUAD)]).then_inc(idx_staged, 1)
                    wait_alone(pool, idx_staged, (EGROUPS + NGROUPS) * s + g + 1, pool_passed)
                    if s < FINAL:
                        wait_alone(pool, msg_made, EGROUPS * s + g - 1, pool_passed)
                    else:
                        wait_alone(pool, seg_turned, g - 1, pool_passed)
                    for c in range(QUAD):
                        gather(x if s == 0 else nodes, idx[:, p, c:c + 1], got[:, p, c, :], sp_got[p])

                if s > 0:
                    for p in range(2):
                        pool.wait_ge(nodes_stored[p], 16 * ND * s)
                else:
                    pool.wait_ge(prep, 3)
                over_groups(pool, 0, EGROUPS, sparse_gather)
                for p in range(2):
                    pool.wait_ge(sp_got[p], 16 * QUAD * NS[p] * (s + 1))

                if s == 0:
                    pool.wait_ge(tables_stored, 32)
                    pool.wait_ge(prep, 10)

                    def scatter(k, p):
                        wait_alone(pool, rows_scattered[p], 16 * QUAD * k, pool_passed)
                        at = bass.ds((2 * k + p) * QUAD, QUAD)
                        nc.gpsimd.tensor_copy(row_stage[:, p, :], row_i[:, at]).then_inc(stage_copied, 1)
                        nc.gpsimd.tensor_copy(node_stage[:, p, :], node_i[:, at]).then_inc(stage_copied, 1)
                        wait_alone(pool, stage_copied, 2 * (2 * k + p + 1), pool_passed)
                        for c in range(QUAD):
                            nc.gpsimd.indirect_dma_start(
                                out=row_of, out_offset=bass.IndirectOffsetOnAxis(ap=node_stage[:, p, c:c + 1], axis=0),
                                in_=row_stage[:, p, c:c + 1], in_offset=None, bounds_check=NP - 1,
                                oob_is_err=False).then_inc(rows_scattered[p], 16)

                    over_groups(pool, 0, EGROUPS, scatter)

                def dense_gather(k, p):
                    g, u = 2 * k + p, ND * s + k
                    wait_alone(pool, dn_got[p], 16 * QUAD * u, pool_passed)
                    nc.gpsimd.tensor_copy(idx[:, p, :], row_idx[:, bass.ds(g * QUAD, QUAD)]).then_inc(idx_staged, 1)
                    wait_alone(pool, idx_staged, (EGROUPS + NGROUPS) * s + EGROUPS + g + 1, pool_passed)
                    if s < FINAL:
                        wait_alone(pool, turned, NGROUPS * s + g - 1, pool_passed)
                    else:
                        wait_alone(pool, ln, ln_read(s, k, p, 2), pool_passed)
                    for t in range(QUAD):
                        gather(sums, idx[:, p, t:t + 1], got[:, p, t, :], dn_got[p])

                pool.wait_ge(row_idx_loaded, 16)
                for p in range(2):
                    pool.wait_ge(sums_stored[p], 16 * NS[p] * (s + 1))
                pool.wait_ge(runs_stored, 16 * (s + 1))
                over_groups(pool, 0, NGROUPS, dense_gather)
                for p in range(2):
                    pool.wait_ge(dn_got[p], 16 * QUAD * ND * (s + 1))

        @block.tensor
        def _(pe):
            pe.wait_ge(prep, 1)
            pe.wait_ge(const_made, 8)
            for i, ps in enumerate((ps_in, ps_agg, ps_out)):
                for h in range(2):
                    last = nc.tensor.transpose(ps[:, 0, h * CH:(h + 1) * CH], rawf[:, i, h, :], ident[0:CH, 0:CH])
            last.then_inc(prep_pe, 1)
            pe.wait_ge(prep, 2)
            nc.tensor.matmul(ps_back[:, 0, 0:CHUNKS], sel_last[:, :], dcol[:, :], start=True, stop=True)
            nc.tensor.matmul(ps_back[:, 1, 0:CHUNKS], sel_first[:, :], dcol[:, :], start=True,
                             stop=True).then_inc(prep_pe, 1)
            pe.wait_ge(loaded, 16 * 8)

            def sparse(s):
                def turn_edges(k, p):
                    g, u = 2 * k + p, NS[p] * s + k
                    if s == 0:
                        pe.wait_ge(e_loaded[p], 16 * (u + 1))
                        wait(pe, e_turned_out, H * g)
                        for h in range(H):
                            for c in range(QUAD):
                                last = nc.tensor.transpose(
                                    ps_in[:, h, c * P:(c + 1) * P],
                                    ein[:, p, c * D + h * P:c * D + (h + 1) * P], ident[:, :])
                    else:
                        pe.wait_ge(e_shifted, EGROUPS * (s - 1) + g + 1)
                        wait(pe, msg_summed, EGROUPS * s + g)
                        for c in range(QUAD):
                            for h in range(H):
                                last = nc.tensor.transpose(as_rows(ps_in)[:, c, h * P:(h + 1) * P],
                                                           tin[:, p, h, c * P:(c + 1) * P], ident[:, :])
                    last.then_inc(e_turned, 1)

                def update_edges(k, p):
                    g = 2 * k + p
                    G = EGROUPS * s + g
                    if s == 0:
                        pe.wait_ge(e_turned_out, H * (g + 1))
                    src_t = tin[:, p, :, :] if s == 0 else ein[:, p, :].rearrange("p (h j) -> p h j", h=H)
                    for ho in range(H):
                        wait(pe, e_updated, H * G - H + 1 + ho)
                        for h in range(H):
                            last = nc.tensor.matmul(ps_out[:, ho, :], we[:, s, h, ho * P:(ho + 1) * P], src_t[:, h, :],
                                                    start=(h == 0), stop=(h == H - 1))
                        last.then_inc(e_product, 1)

                def sum_messages(k, p):
                    g = 2 * k + p
                    pe.wait_ge(same_made, EGROUPS * s + g + 1)
                    pe.wait_ge(msg_made, EGROUPS * s + g + 1)
                    wait(pe, sums_out, EGROUPS * s + g)
                    for c in range(QUAD):
                        last = nc.tensor.matmul(as_rows(ps_agg)[:, c, :], same[:, p, c, :], mid[:, p, c, :],
                                                start=True, stop=True)
                    last.then_inc(sums_made, 1)

                def step(k, p):
                    turn_edges(k, p)
                    if s == 0:
                        sum_messages(k, p)
                        update_edges(k, p)
                    else:
                        if s < LAYERS:
                            update_edges(k, p)
                        sum_messages(k, p)

                over_groups(pe, 0, EGROUPS, step)

            def sparse_final():
                s = FINAL

                def sum_turned(k, p):
                    g, u = 2 * k + p, NS[p] * s + k
                    pe.wait_ge(sp_got[p], 16 * QUAD * (u + 1))
                    pe.wait_ge(same_made, EGROUPS * s + g + 1)
                    wait(pe, seg_turned_out, H * g)
                    for c in range(QUAD):
                        for h in range(H):
                            last = nc.tensor.matmul(ps_in[:, h, c * P:(c + 1) * P], got[:, p, c, h * P:(h + 1) * P],
                                                    same[:, p, c, :], start=True, stop=True)
                    last.then_inc(seg_turned, 1)

                def times_m(k, p):
                    g = 2 * k + p
                    pe.wait_ge(seg_turned_out, H * (g + 1))
                    wait(pe, sums_out, EGROUPS * s + g)
                    for c in range(QUAD):
                        for h in range(H):
                            last = nc.tensor.matmul(as_rows(ps_agg)[:, c, :], tin[:, p, h, c * P:(c + 1) * P],
                                                    m1[:, h, :], start=(h == 0), stop=(h == H - 1))
                    last.then_inc(sums_made, 1)

                def step(k, p):
                    sum_turned(k, p)
                    times_m(*before(k, p))

                sum_turned(0, 0)
                over_groups(pe, 1, EGROUPS, step)
                times_m((EGROUPS - 1) // 2, (EGROUPS - 1) % 2)

            def runs(s):
                pe.wait_ge(runs_loaded, 32 * (s + 1))
                pe.wait_ge(links_made, 2)
                pe.wait_ge(sums_out, EGROUPS * (s + 1))
                for ho in range(2):
                    for h in range(2):
                        last = nc.tensor.matmul(ps_agg[0:CH, ho, 0:D], links[:, h, ho * CH:(ho + 1) * CH],
                                                run_last[:, h, :], start=(h == 0), stop=(h == 1))
                last.then_inc(runs_product, 1)
                pe.wait_ge(runs_summed, s + 1)

            def dense(d):
                wl = min(d, LAYERS - 1)

                def turn_in(k, p):
                    g, u = 2 * k + p, ND * d + k
                    pe.wait_ge(rows_loaded[p], 16 * (u + 1))
                    wait(pe, scaled, H * (NGROUPS * d + g))
                    for h in range(H):
                        for t in range(QUAD):
                            last = nc.tensor.transpose(ps_in[:, h, t * P:(t + 1) * P],
                                                       rows[:, p, t, h * P:(h + 1) * P], ident[:, :])
                    if d < FINAL:
                        pe.wait_ge(dn_got[p], 16 * QUAD * (u + 1))
                        wait(pe, added, H * (NGROUPS * d + g))
                        for h in range(H):
                            for t in range(QUAD):
                                last = nc.tensor.transpose(ps_agg[:, h, t * P:(t + 1) * P],
                                                           got[:, p, t, h * P:(h + 1) * P], ident[:, :])
                    last.then_inc(turned, 1)

                def main(k, p):
                    g = 2 * k + p
                    G = NGROUPS * d + g
                    if d < FINAL:
                        pe.wait_ge(added, H * (G + 1))
                        for ho in range(H):
                            wait(pe, activated, H * G - H + 1 + ho)
                            for h in range(H):
                                last = nc.tensor.matmul(ps_out[:, ho, :], wc[:, wl, h, ho * P:(ho + 1) * P],
                                                        tin[:, p, h, :], start=(h == 0), stop=(h == H - 1))
                            last.then_inc(product, 1)
                    else:
                        pe.wait_ge(scaled, H * (G + 1))
                        wait(pe, ln, ln_read(d, k, p, 1) - 1)
                        for t in range(QUAD):
                            for h in range(H):
                                last = nc.tensor.matmul(as_rows(ps_out)[:, t, :], tin[:, p, h, t * P:(t + 1) * P],
                                                        w1[:, h, :], start=(h == 0), stop=(h == H - 1))
                        last.then_inc(product, 1)

                def turn_back(k, p):
                    g = 2 * k + p
                    pe.wait_ge(activated, H * (NGROUPS * d + g + 1))
                    if d < LAST:
                        wait(pe, rows_out, NGROUPS * d + g)
                    elif not isinstance(g, int) or g > 0:
                        wait(pe, ln, ln_read(d, k, p, 1))
                    for t in range(QUAD):
                        for h in range(H):
                            last = nc.tensor.transpose(as_rows(ps_back)[:, t, h * P:(h + 1) * P],
                                                       tout[:, p, h, t * P:(t + 1) * P], ident[:, :])
                    last.then_inc(back, 1)

                def step(k, p):
                    turn_in(*after(k, p))
                    main(k, p)
                    if d < FINAL and not (isinstance(k, int) and k == 0 and p == 0):
                        turn_back(*before(k, p))

                end = NGROUPS - 1
                turn_in(0, 0)
                over_groups(pe, 0, end, step)
                main(end // 2, end % 2)
                if d < FINAL:
                    turn_back((end - 1) // 2, (end - 1) % 2)
                    turn_back(end // 2, end % 2)

            for s in range(SPARSE):
                sparse_final() if s == FINAL else sparse(s)
                runs(s)
                dense(s)
                if s < LAYERS:
                    pe.wait_ge(bn, BN_STEPS * (s + 1))
                    for h in range(H):
                        last = nc.tensor.matmul(ps_back[:, 0, h * P:(h + 1) * P], ones[:, :], diag[:, h, :],
                                                start=True, stop=True)
                    last.then_inc(bn_row, 1)
                    pe.wait_ge(bn_row_out, s + 1)

        @block.scalar
        def _(act):
            def sparse(s):
                def step(k, p):
                    g, u = 2 * k + p, NS[p] * s + k
                    G = EGROUPS * s + g

                    def messages():
                        act.wait_ge(msg_summed, G + 1)
                        wait(act, sums_made, G - 1)
                        nc.scalar.activation(mid[:, p, :, :], got[:, p, :, :], ACT.Relu).then_inc(msg_made, 1)

                    def updates():
                        for ho in range(H):
                            act.wait_ge(e_product, H * G + ho + 1)
                            wait(act, e_stored[p], 16 * u)
                            nc.scalar.activation(tout[:, p, ho, :], ps_out[:, ho, :], ACT.Relu,
                                                 bias=be[:, s, ho:ho + 1]).then_inc(e_updated, 1)

                    def results():
                        act.wait_ge(sums_made, G + 1)
                        wait(act, sums_stored[p], 16 * u)
                        nc.scalar.copy(res[:, p, :, :], as_rows(ps_agg)).then_inc(sums_out, 1)

                    if s == FINAL:
                        results()
                        return
                    if s == 0:
                        for h in range(H):
                            act.wait_ge(e_turned, G + 1)
                            wait(act, e_product, H * (G - 1))
                            nc.scalar.copy(tin[:, p, h, :], ps_in[:, h, :]).then_inc(e_turned_out, 1)
                        messages()
                        results()
                        updates()
                    else:
                        messages()
                        if s < LAYERS:
                            updates()
                        results()

                def turned_sums(k, p):
                    g = 2 * k + p
                    for h in range(H):
                        act.wait_ge(seg_turned, g + 1)
                        wait(act, sums_made, EGROUPS * s + g - 1)
                        nc.scalar.copy(tin[:, p, h, :], ps_in[:, h, :]).then_inc(seg_turned_out, 1)

                def final_step(k, p):
                    turned_sums(k, p)
                    step(*before(k, p))

                if s == FINAL:
                    turned_sums(0, 0)
                    over_groups(act, 1, EGROUPS, final_step)
                    step((EGROUPS - 1) // 2, (EGROUPS - 1) % 2)
                else:
                    over_groups(act, 0, EGROUPS, step)

            def dense(d):
                wl = min(d, LAYERS - 1)

                def scale_in(k, p):
                    G = NGROUPS * d + 2 * k + p
                    act.wait_ge(turned, G + 1)
                    for h in range(H):
                        if d == FINAL:
                            wait(act, product, H * NGROUPS * FINAL + (2 * k + p) - 1)
                            nc.scalar.copy(tin[:, p, h, :], ps_in[:, h, :]).then_inc(scaled, 1)
                        else:
                            wait(act, product, H * (G - 1))
                            nc.scalar.activation(tin[:, p, h, :], ps_in[:, h, :], ACT.Identity,
                                                 bias=shift[:, h:h + 1], scale=scale[:, h:h + 1]).then_inc(scaled, 1)

                def activate(k, p):
                    g = 2 * k + p
                    G = NGROUPS * d + g
                    for ho in range(H):
                        act.wait_ge(product, H * G + ho + 1)
                        if not isinstance(g, int) or g >= 2:
                            wait(act, back, G - 1)
                            if d < LAYERS:
                                wait(act, counted, H * (G - 1))
                        nc.scalar.activation(tout[:, p, ho, :], ps_out[:, ho, :], ACT.Relu,
                                             bias=bc[:, wl, ho:ho + 1]).then_inc(activated, 1)

                def deviations(k, p):
                    g = NGROUPS * (d - LAST) + 2 * k + p
                    act.wait_ge(ln, LN_STEPS * (g + 1))
                    nc.scalar.activation(ln_std[:, p, :], ln_mv[:, p, :, 1], ACT.Sqrt, bias=eps[:, 0:1]).then_inc(
                        ln_std_made, 1)

                def step(k, p):
                    first = isinstance(k, int) and k == 0 and p == 0
                    scale_in(*after(k, p))
                    if d < FINAL:
                        activate(k, p)
                    if d == LAST and not first:
                        deviations(*before(k, p))
                    if d == FINAL:
                        deviations(k, p)

                end = NGROUPS - 1
                if d == 0:
                    act.wait_ge(prep, 13)
                elif d < FINAL:
                    act.wait_ge(bn, BN_STEPS * min(d, LAYERS))
                scale_in(0, 0)
                over_groups(act, 0, end, step)
                if d < FINAL:
                    activate(end // 2, end % 2)
                if d == LAST:
                    deviations((end - 1) // 2, (end - 1) % 2)
                if d >= LAST:
                    deviations(end // 2, end % 2)

            act.wait_ge(loaded, 16 * 8)
            for s in range(SPARSE):
                if 0 < s < LAYERS:
                    act.wait_ge(back, NGROUPS * s)
                    act.wait_ge(counted, H * NGROUPS * s)
                sparse(s)
                if s < LAYERS:
                    for p in range(2):
                        act.wait_ge(e_stored[p], 16 * NS[p] * (s + 1))
                dense(s)
                if s < LAYERS:
                    act.wait_ge(bn, BN_STEPS * s + 1)
                    nc.scalar.activation(bn_std[:, :], mv[:, :, 1], ACT.Sqrt, bias=eps[:, 0:1]).then_inc(bn_std_made, 1)
                    act.wait_ge(bn_row, s + 1)
                    nc.scalar.copy(scale_row[:, :], ps_back[:, 0, 0:D]).then_inc(bn_row_out, 1)

        @block.vector
        def _(dve):
            dve.wait_ge(raw_loaded, 48)
            nc.vector.tensor_copy(rawf[:, :, :, :], raw[:, :, :, :]).then_inc(prep, 1)
            dve.wait_ge(prep_pe, 1)
            nc.vector.tensor_copy(dcol[:, :], ps_in[:, 0, 0:CHUNKS]).then_inc(prep, 1)
            nc.vector.tensor_copy(src_i[:, :], ps_out[:, 0, 0:CHUNKS]).then_inc(prep, 1)
            nc.vector.tensor_copy(dnext[:, :], ps_agg[:, 0, 0:CHUNKS]).then_inc(prep, 1)
            nc.vector.memset(prev_last[:, 0:1], -1.0).then_inc(prep, 1)
            dve.wait_ge(prep_pe, 2)
            nc.vector.tensor_copy(prev_last[:, 1:CHUNKS], ps_back[:, 0, 0:CHUNKS - 1]).then_inc(prep, 1)
            nc.vector.tensor_copy(first_row[:, :], ps_back[0:CH, 1, 0:CHUNKS]).then_inc(prep, 1)
            dve.wait_ge(const_made, 8)
            nc.vector.tensor_copy(j_f[:, :], j_i[:, :]).then_inc(prep, 1)
            dve.wait_ge(prep, 8)
            nc.vector.tensor_tensor(flag[:, :], prev_last[:, :], dcol[:, :], ALU.is_equal).then_inc(steps, 1)
            nc.vector.tensor_tensor(span_f[:, :], span_i[:, :], j_f[:, :], ALU.subtract).then_inc(steps, 1)
            dve.wait_ge(steps, 2)
            nc.vector.tensor_tensor(span_f[:, :], span_f[:, :], flag[:, :], ALU.mult).then_inc(steps, 1)
            dve.wait_ge(steps, 3)
            nc.vector.tensor_tensor(row_i[:, :], span_f[:, :], j_f[:, :], ALU.add).then_inc(steps, 1)
            nc.vector.tensor_tensor(flag[:, :], dnext[:, :], dcol[:, :], ALU.is_equal).then_inc(steps, 1)
            dve.wait_ge(steps, 5)
            nc.vector.scalar_tensor_tensor(out=node_i[:, :], in0=flag[:, :], scalar=float(PAD_DST), in1=dcol[:, :],
                                           op0=ALU.mult, op1=ALU.add).then_inc(steps, 1)
            nc.vector.tensor_scalar(links[:, 0, :], first_row[:, :], rawf[:, 0, 0, P - 1:P], None, ALU.is_equal).then_inc(steps, 1)
            nc.vector.tensor_scalar(links[:, 1, :], first_row[:, :], rawf[:, 0, 1, P - 1:P], None, ALU.is_equal).then_inc(steps, 1)
            dve.wait_ge(steps, 8)
            nc.vector.memset(tmp[:, :], 0.0).then_inc(prep, 1)
            nc.vector.memset(mv[:, :, :], 0.0).then_inc(prep, 1)
            nc.vector.memset(scale[:, :], 1.0).then_inc(prep, 1)
            nc.vector.memset(shift[:, :], 0.0).then_inc(prep, 1)
            nc.vector.memset(eps[:, :], EPS).then_inc(prep, 1)
            dve.wait_ge(loaded, 16 * 8)
            dve.wait_ge(prep, 13)

            def sparse(s):
                def find_same(k, p):
                    g, u = 2 * k + p, NS[p] * s + k
                    dve.wait_ge(drow_loaded[p], 16 * (u + 1))
                    if s < FINAL:
                        wait(dve, sums_made, EGROUPS * s + g - 1)
                    else:
                        wait(dve, seg_turned, g - 1)
                    nc.vector.tensor_tensor(
                        same[:, p, :, :], drow[:, p, :].rearrange("p (c j) -> p c j", c=QUAD),
                        dcol[:, bass.ds(g * QUAD, QUAD)].unsqueeze(2).to_broadcast([P, QUAD, P]),
                        ALU.is_equal).then_inc(same_made, 1)

                def shift_edges(k, p):
                    g, u = 2 * k + p, NS[p] * s + k
                    dve.wait_ge(e_loaded[p], 16 * (u + 1))
                    wait(dve, e_turned, EGROUPS * s + g - 1)
                    for h in range(H):
                        last = nc.vector.tensor_scalar(tin[:, p, h, :], ein[:, p, h * QUAD * P:(h + 1) * QUAD * P],
                                                       shift[:, h:h + 1], None, ALU.add)
                    last.then_inc(e_shifted, 1)

                def messages(k, p):
                    g, u = 2 * k + p, NS[p] * s + k
                    G = EGROUPS * s + g
                    dve.wait_ge(sp_got[p], 16 * QUAD * (u + 1))
                    if s == 0:
                        dve.wait_ge(e_loaded[p], 16 * (u + 1))
                        nc.vector.tensor_tensor(got[:, p, :, :], got[:, p, :, :],
                                                ein[:, p, :].rearrange("p (c f) -> p c f", f=D),
                                                ALU.add).then_inc(msg_summed, 1)
                        return
                    nc.vector.tensor_tensor(got[:, p, :, :], got[:, p, :, :],
                                            scale_row[:, :].unsqueeze(1).to_broadcast([P, QUAD, D]),
                                            ALU.mult).then_inc(got_scaled, 1)
                    dve.wait_ge(got_scaled, G - EGROUPS + 1)
                    dve.wait_ge(e_turned, G + 1)
                    nc.vector.tensor_tensor(got[:, p, :, :], as_rows(ps_in), got[:, p, :, :],
                                            ALU.add).then_inc(msg_summed, 1)

                def step(k, p):
                    if s < FINAL:
                        messages(k, p)
                    if 0 < s < FINAL:
                        shift_edges(*after(k, p))
                    find_same(*after(k, p))

                if 0 < s < FINAL:
                    dve.wait_ge(bn_row_out, s if s < LAYERS else LAYERS)
                    shift_edges(0, 0)
                find_same(0, 0)
                end = EGROUPS - 1
                over_groups(dve, 0, end, step)
                if s < FINAL:
                    messages(end // 2, end % 2)

            def runs(s):
                dve.wait_ge(runs_product, s + 1)
                dve.wait_ge(runs_loaded, 32 * (s + 1))
                if s > 0:
                    dve.wait_ge(runs_stored, 16 * s)
                nc.vector.tensor_tensor(run_sum[:, :, :], ps_agg[0:CH, :, 0:D], run_first[:, :, :],
                                        ALU.add).then_inc(runs_summed, 1)

            def ln_variance(d, k, p):
                done = ln_read(d, k, p)
                dve.wait_ge(ln, done)
                for t in range(QUAD):
                    last = nc.vector.bn_stats(ln_stats[:, p, t, :], mid[:, p, t, :])
                last.then_inc(ln, 1)
                wait_alone(dve, ln, done + 1, dve_passed)
                for t in range(QUAD):
                    last = nc.vector.bn_aggr(ln_mv[:, p, t, :], ln_stats[:, p, t, :])
                last.then_inc(ln, 1)

            def ln_rows(d, k, p):
                g = NGROUPS * (d - LAST) + 2 * k + p
                dve.wait_ge(ln_std_made, g + 1)
                nc.vector.reciprocal(ln_rstd[:, p, :], ln_std[:, p, :]).then_inc(ln_rstd_made, 1)
                dve.wait_ge(ln_rstd_made, g + 1)
                wait(dve, nodes_stored[p], 16 * (ND * d + k))
                for t in range(QUAD):
                    last = nc.vector.tensor_scalar(res[:, p, t, :], mid[:, p, t, :], ln_mv[:, p, t, 0:1],
                                                   ln_rstd[:, p, t:t + 1], ALU.subtract, ALU.mult)
                last.then_inc(ln_out, 1)

            def dense(d):
                def add_sums(k, p):
                    G = NGROUPS * d + 2 * k + p
                    for h in range(H):
                        dve.wait_ge(scaled, H * G + h + 1)
                        nc.vector.tensor_tensor(tin[:, p, h, :], ps_agg[:, h, :], tin[:, p, h, :],
                                                ALU.add).then_inc(added, 1)

                def count(k, p, full):
                    G = NGROUPS * d + 2 * k + p
                    for h in range(H):
                        dve.wait_ge(activated, H * G + h + 1)
                        to = stats[:, h, bass.ds(2 * k + p, 1), :].rearrange("p o s -> p (o s)")
                        if full:
                            of = tout[:, p, h, :]
                        else:
                            of = tout[:, p, h, :].rearrange("p (t j) -> p t j", j=P)[:, :, 0:P - 1]
                        nc.vector.bn_stats(to, of).then_inc(counted, 1)

                def copy_rows(k, p):
                    g, u = 2 * k + p, ND * d + k
                    dve.wait_ge(back, NGROUPS * d + g + 1)
                    wait(dve, nodes_stored[p], 16 * u)
                    nc.vector.tensor_copy(res[:, p, :, :], as_rows(ps_back)).then_inc(rows_out, 1)

                def last_conv_rows(k, p):
                    g = 2 * k + p
                    wait(dve, ln_out, NGROUPS * (d - LAST) + g - 1)
                    dve.wait_ge(x_loaded[p], 16 * (k + 1))
                    dve.wait_ge(back, NGROUPS * d + g + 1)
                    nc.vector.scalar_tensor_tensor(
                        out=mid[:, p, :, :], in0=ein[:, p, :].rearrange("p (t f) -> p t f", f=D), scalar=2.0,
                        in1=as_rows(ps_back), op0=ALU.mult, op1=ALU.add).then_inc(ln, 2)
                    ln_variance(d, k, p)
                    if not isinstance(g, int) or g > 0:
                        ln_rows(d, *before(k, p))

                def final_rows(k, p):
                    g, u = 2 * k + p, ND * d + k
                    wait(dve, ln_out, NGROUPS * (d - LAST) + g - 1)
                    dve.wait_ge(dn_got[p], 16 * QUAD * (u + 1))
                    dve.wait_ge(product, H * NGROUPS * FINAL + g + 1)
                    nc.vector.tensor_tensor(mid[:, p, :, :], as_rows(ps_out), got[:, p, :, :],
                                            ALU.add).then_inc(ln, 1)
                    dve.wait_ge(ln, ln_read(d, k, p) - 1)
                    nc.vector.scalar_tensor_tensor(out=mid[:, p, :, :], in0=mid[:, p, :, :], scalar=0.0,
                                                   in1=rows[:, p, :, :], op0=ALU.max, op1=ALU.add).then_inc(ln, 1)
                    ln_variance(d, k, p)
                    if not isinstance(g, int) or g > 0:
                        ln_rows(d, *before(k, p))

                def step(full):
                    def run(k, p):
                        add_sums(*after(k, p))
                        if d < LAYERS:
                            count(k, p, full)
                        if not (isinstance(k, int) and k == 0 and p == 0):
                            (copy_rows if d < LAST else last_conv_rows)(*before(k, p))
                    return run

                end = NGROUPS - 1
                if d == FINAL:
                    over_groups(dve, 0, NGROUPS, final_rows)
                    ln_rows(d, end // 2, end % 2)
                    return
                add_sums(0, 0)
                over_groups(dve, 0, FULL, step(True))
                over_groups(dve, FULL, end, step(False))
                if d < LAYERS:
                    count(end // 2, end % 2, False)
                for g in (end - 1, end):
                    (copy_rows if d < LAST else last_conv_rows)(g // 2, g % 2)
                if d == LAST:
                    ln_rows(d, end // 2, end % 2)

            def batch_norm(d):
                done = BN_STEPS * d
                dve.wait_ge(counted, H * NGROUPS * (d + 1))
                for h in range(H):
                    last = nc.vector.bn_aggr(mv[:, h, :], stats[:, h, :, :].rearrange("p g s -> p (g s)"))
                last.then_inc(bn, 1)
                dve.wait_ge(bn, done + 1)
                dve.wait_ge(bn_std_made, d + 1)
                nc.vector.reciprocal(rstd[:, :], bn_std[:, :]).then_inc(bn, 1)
                dve.wait_ge(bn, done + 2)
                nc.vector.tensor_tensor(scale[:, :], rstd[:, :], gam[:, d, :], ALU.mult).then_inc(bn, 1)
                dve.wait_ge(bn, done + 3)
                nc.vector.tensor_tensor(tmp[:, :], mv[:, :, 0], scale[:, :], ALU.mult).then_inc(bn, 1)
                for h in range(H):
                    last = nc.vector.tensor_scalar(diag[:, h, :], ident[:, :], scale[:, h:h + 1], None, ALU.mult)
                last.then_inc(bn, 1)
                dve.wait_ge(bn, done + 5)
                nc.vector.tensor_tensor(shift[:, :], bet[:, d, :], tmp[:, :], ALU.subtract).then_inc(bn, 1)
                dve.wait_ge(bn, done + 6)

            for s in range(SPARSE):
                sparse(s)
                runs(s)
                dense(s)
                if s < LAYERS:
                    batch_norm(s)


def kernel(x, src, dst, edge_attr_256, L0_gnn_W_conv, L0_gnn_b_conv, L0_gnn_W_edge, L0_gnn_b_edge, L0_gnn_gamma,
           L0_gnn_beta, L1_gnn_W, L1_gnn_M):
    import numpy as np
    import concourse.bacc as bacc
    from concourse.bass_utils import run_bass_kernel_spmd

    def pad(a, rows, value=0):
        a = np.asarray(a)
        return np.concatenate([a, np.full((rows - a.shape[0],) + a.shape[1:], value, a.dtype)])

    def halves(w):
        w = np.asarray(w)
        lead = w.shape[:-2]
        w = w.reshape(lead + (H, P, w.shape[-1]))
        return np.ascontiguousarray(np.moveaxis(w, -2, 0))

    def columns(b):
        b = np.asarray(b)
        return np.ascontiguousarray(np.moveaxis(b.reshape(b.shape[0], H, P), -1, 0))

    dst_padded = pad(pad(dst, EP, PAD_DST), EP + 1, END_DST)
    arrays = {
        "x": pad(x, NP), "src": pad(src, EP), "dst": dst_padded, "edge": pad(edge_attr_256, EP),
        "w_conv": halves(L0_gnn_W_conv), "b_conv": columns(L0_gnn_b_conv), "w_edge": halves(L0_gnn_W_edge),
        "b_edge": columns(L0_gnn_b_edge), "gamma": columns(L0_gnn_gamma), "beta": columns(L0_gnn_beta),
        "l1_w": halves(L1_gnn_W), "l1_m": halves(L1_gnn_M),
    }
    nc = bacc.Bacc("TRN2", target_bir_lowering=False, num_devices=1)
    feeds, args = {}, {}
    for name, a in arrays.items():
        feeds[f"in_{name}"] = a
        args[name] = nc.dram_tensor(f"in_{name}", a.shape, mybir.dt.from_np(a.dtype), kind="ExternalInput").ap()
    out = nc.dram_tensor("out_nodes", (NP, D), F32, kind="ExternalOutput").ap()
    gnn_kernel(nc, **args, out=out)
    got = run_bass_kernel_spmd(nc, [feeds], core_ids=[0])
    return got.results[0]["out_nodes"][0:N]
```

```python
from contextlib import ExitStack

import concourse.bass as bass
from concourse import mybir

ALU = mybir.AluOpType
ACT = mybir.ActivationFunctionType
F32 = mybir.dt.float32
I32 = mybir.dt.int32
U8 = mybir.dt.uint8

P = 128
D = 256
H = D // P
QUAD = 4
SLOTS = 4
N = 50000
E = 25000
LAYERS = 4
EPS = 1e-5

CHUNKS = -(-E // P)
EP = CHUNKS * P
EGROUPS = CHUNKS // QUAD
CH = CHUNKS // 2
NGROUPS = -(-N // (P * QUAD))
TILES = NGROUPS * QUAD
NP = TILES * P
FULL = (N - (P - 1) * TILES) // QUAD
PAD_DST = 1 << 20
END_DST = 1 << 21
SPAN = EP
ZERO = SPAN + CHUNKS
SUMS = ZERO + P
assert CHUNKS % QUAD == 0 and (N - (P - 1) * TILES) % QUAD == 0


def over_groups(eng, first, last, step):
    g = first
    while g < last and (g < SLOTS or g % SLOTS):
        step(*place(g))
        g += 1
    rounds = (last - g) // SLOTS
    if rounds > 0:
        with eng.Fori(g // SLOTS, g // SLOTS + rounds) as k:
            for q in range(SLOTS):
                step(k, q)
        g += SLOTS * rounds
    while g < last:
        step(*place(g))
        g += 1


def place(g):
    return g // SLOTS, g % SLOTS


def ahead(k, q, by=1):
    turn, q = (q + by) // SLOTS, (q + by) % SLOTS
    return (k + turn if turn > 0 else k - -turn if turn < 0 else k), q


def behind(k, q, by=1):
    return ahead(k, q, -by)


def number(k, q):
    return SLOTS * k + q, q % 2, SLOTS // 2 * k + q // 2


def starts(k, q, groups):
    return isinstance(k, int) and SLOTS * k + q < groups


def wait(eng, sem, value):
    if not isinstance(value, int) or value > 0:
        eng.wait_ge(sem, value)


def wait_alone(eng, sem, value, passed):
    wait(eng, sem, value)
    if not isinstance(value, int):
        eng.sem_inc(passed, 1)


def gnn_kernel(nc, x, src, dst, edge, w_conv, b_conv, w_edge, b_edge, gamma, beta, l1_w, l1_m, out):
    ctx = ExitStack()
    with ctx:
        def sb(name, shape, dt=F32):
            return ctx.enter_context(nc.sbuf_tensor(name, shape, dt))

        def sem(name):
            return ctx.enter_context(nc.semaphore(name))

        def slots(name, n=2):
            return [sem(f"{name}{i}") for i in range(n)]

        nodes = nc.dram_tensor("nodes", [NP, D], F32).ap()
        sums = nc.dram_tensor("sums", [SUMS, D], F32).ap()
        edge_t = nc.dram_tensor("edge_t", [EGROUPS, P, H * QUAD * P], F32).ap()
        row_of = nc.dram_tensor("row_of", [NP, 1], I32).ap()

        def tiles(ap):
            return ap.rearrange("(p t) f -> p t f", p=P)

        nodes_v, x_v, out_v = tiles(nodes), tiles(x), tiles(out)
        row_of_v = row_of.rearrange("(p t) o -> p (t o)", p=P)
        sums_v = sums[0:EP, :].rearrange("(c p) f -> p c f", p=P)
        edge_v = edge.rearrange("(c p) f -> p c f", p=P)
        dst_groups = dst[0:EP].rearrange("(g j) -> g j", j=QUAD * P)

        def chunk_rows(ap):
            return ap.rearrange("(h q p) -> q h p", h=2, q=CH)

        wc = sb("wc", [P, LAYERS, H, D])
        we = sb("we", [P, LAYERS, H, D])
        w1 = sb("w1", [P, H, D])
        m1 = sb("m1", [P, H, D])
        bc = sb("bc", [P, LAYERS, H])
        be = sb("be", [P, LAYERS, H])
        gam = sb("gam", [P, LAYERS, H])
        bet = sb("bet", [P, LAYERS, H])
        ones = sb("ones", [P, P])
        ident = sb("ident", [P, P])
        sel_last = sb("sel_last", [P, P])
        sel_first = sb("sel_first", [P, P])

        raw = sb("raw", [CH, 3, 2, P], I32)
        rawf = sb("rawf", [CH, 3, 2, P])
        dcol = sb("dcol", [P, CHUNKS])
        dnext = sb("dnext", [P, CHUNKS])
        src_i = sb("src_i", [P, CHUNKS], I32)
        prev_last = sb("prev_last", [P, CHUNKS])
        first_row = sb("first_row", [CH, CHUNKS])
        links = sb("links", [CH, 2, CHUNKS])
        j_i = sb("j_i", [P, CHUNKS], I32)
        span_i = sb("span_i", [P, CHUNKS], I32)
        j_f = sb("j_f", [P, CHUNKS])
        span_f = sb("span_f", [P, CHUNKS])
        flag = sb("flag", [P, CHUNKS])
        row_i = sb("row_i", [P, CHUNKS], I32)
        node_i = sb("node_i", [P, CHUNKS], I32)
        zero_rows = sb("zero_rows", [P, TILES], I32)
        row_stage = sb("row_stage", [P, 2, QUAD], I32)
        node_stage = sb("node_stage", [P, 2, QUAD], I32)

        stats = sb("stats", [P, H, NGROUPS, 6])
        mv = sb("mv", [P, H, 2])
        rstd = sb("rstd", [P, H])
        scale = sb("scale", [P, H])
        shift = sb("shift", [P, H])
        tmp = sb("tmp", [P, H])
        diag = sb("diag", [P, H, P])
        scale_row = sb("scale_row", [P, D])

        idx = sb("idx", [P, SLOTS, QUAD], I32)
        row_idx = sb("row_idx", [P, TILES], I32)
        got = sb("got", [P, SLOTS, QUAD, D])
        ein = sb("ein", [P, 2, QUAD * D])
        rows = sb("rows", [P, SLOTS, QUAD, D])
        tin = sb("tin", [P, 2, H, QUAD * P])
        tout = sb("tout", [P, 2, H, QUAD * P])
        mid = sb("mid", [P, 2, QUAD, D])
        res = sb("res", [P, 2, QUAD, D])
        drow = sb("drow", [P, 2, QUAD * P], I32)
        same = sb("same", [P, 2, QUAD, P])
        same_all = sb("same_all", [P, CHUNKS, P], U8)
        ln_stats = sb("ln_stats", [P, 2, QUAD, 6])
        ln_mv = sb("ln_mv", [P, 2, QUAD, 2])
        ln_std = sb("ln_std", [P, 2, QUAD])
        eps = sb("eps", [P, 1])
        bn_std = sb("bn_std", [P, H])
        ln_rstd = sb("ln_rstd", [P, 2, QUAD])
        run_last = sb("run_last", [CH, 2, D])
        run_first = sb("run_first", [CH, 2, D])
        run_sum = sb("run_sum", [CH, 2, D])

        def bank2(name):
            return ctx.enter_context(nc.psum_tensor(name, [P, H, QUAD * P], F32))

        ps_in, ps_agg, ps_out, ps_back = (bank2(n) for n in ("ps_in", "ps_agg", "ps_out", "ps_back"))

        ps_final = ps_out, ps_back

        def as_rows(ps):
            return ps[:, :, :].rearrange("p h (k f) -> p (h k) f", f=D)

        loaded = sem("loaded")
        raw_loaded = sem("raw_loaded")
        const_made = sem("const_made")
        prep = sem("prep")
        prep_pe = sem("prep_pe")
        links_made = sem("links_made")
        tables_stored = sem("tables_stored")
        stage_copied = sem("stage_copied")
        row_idx_loaded = sem("row_idx_loaded")
        idx_staged = sem("idx_staged")
        rows_scattered = slots("rows_scattered")

        sp_got = slots("sp_got", SLOTS)
        e_loaded, drow_loaded = map(slots, ("e_loaded", "drow_loaded"))
        e_shifted = sem("e_shifted")
        same_made = sem("same_made")
        same_kept = sem("same_kept")
        got_scaled = sem("got_scaled")
        msg_summed = sem("msg_summed")
        msg_made = sem("msg_made")
        e_turned = sem("e_turned")
        e_turned_out = sem("e_turned_out")
        e_product = sem("e_product")
        e_updated = sem("e_updated")
        sums_made = sem("sums_made")
        sums_out = sem("sums_out")
        sums_stored, e_stored = map(slots, ("sums_stored", "e_stored"))
        seg_turned = sem("seg_turned")
        seg_turned_out = sem("seg_turned_out")
        runs_loaded = sem("runs_loaded")
        runs_product = sem("runs_product")
        runs_summed = sem("runs_summed")
        runs_stored = sem("runs_stored")

        rows_loaded, dn_got = slots("rows_loaded", SLOTS), slots("dn_got", SLOTS)
        nodes_stored, x_loaded = slots("nodes_stored"), slots("x_loaded")
        turned = sem("turned")
        scaled = sem("scaled")
        added = sem("added")
        product = sem("product")
        activated = sem("activated")
        counted = sem("counted")
        back = sem("back")
        rows_out = sem("rows_out")
        ln = sem("ln")
        bn = sem("bn")
        bn_row = sem("bn_row")
        bn_row_out = sem("bn_row_out")
        ln_rstd_made = sem("ln_rstd_made")
        ln_std_made = sem("ln_std_made")
        ln_out = sem("ln_out")
        sp_passed, pool_passed, dve_passed = sem("sp_passed"), sem("pool_passed"), sem("dve_passed")
        bn_std_made = sem("bn_std_made")
        steps = sem("row_steps")

        NS = (EGROUPS + 1) // 2, EGROUPS // 2
        ND = NGROUPS // 2
        NS4 = [len(range(q, EGROUPS, SLOTS)) for q in range(SLOTS)]
        ND4 = [len(range(q, NGROUPS, SLOTS)) for q in range(SLOTS)]
        SPARSE = LAYERS + 2
        LAST = LAYERS
        FINAL = LAYERS + 1

        BN_STEPS = 6
        LN_STEPS = 4

        def ln_read(d, k, q, ago=0):
            return LN_STEPS * (NGROUPS * (d - LAST) + SLOTS * k + q - ago) + 2

        block = ctx.enter_context(nc.Block())

        @block.sync
        def _(sp):
            sp.dma_start(raw[:, 0, :, :], chunk_rows(dst[0:EP])).then_inc(raw_loaded, 16)
            sp.dma_start(raw[:, 1, :, :], chunk_rows(dst[1:EP + 1])).then_inc(raw_loaded, 16)
            sp.dma_start(raw[:, 2, :, :], chunk_rows(src)).then_inc(raw_loaded, 16)
            sp.dma_start(wc[:, :, :, :], w_conv).then_inc(loaded, 16)
            sp.dma_start(we[:, :, :, :], w_edge).then_inc(loaded, 16)
            sp.dma_start(w1[:, :, :], l1_w).then_inc(loaded, 16)
            sp.dma_start(m1[:, :, :], l1_m).then_inc(loaded, 16)
            for to, of in ((bc, b_conv), (be, b_edge), (gam, gamma), (bet, beta)):
                sp.dma_start(to[:, :, :], of).then_inc(loaded, 16)
            sp.wait_ge(const_made, 4)
            sp.dma_start(row_of_v, zero_rows[:, :]).then_inc(tables_stored, 16)
            sp.dma_start(sums[ZERO:ZERO + P, :], res[:, 0, 0, :]).then_inc(tables_stored, 16)
            sp.wait_ge(tables_stored, 32)

            def sparse_load(s, k, q):
                g, p, i = number(k, q)
                u, v = NS[p] * s + i, NS4[q] * s + k
                if s == 0:
                    wait_alone(sp, same_made, g - 1, sp_passed)
                    sp.dma_start(drow[:, p, :], dst_groups[bass.ds(g, 1), :].to_broadcast([P, QUAD * P])).then_inc(
                        drow_loaded[p], 16)
                    if not starts(k, q, 2):
                        wait_alone(sp, e_turned, g - 1, sp_passed)
                        wait_alone(sp, msg_summed, g - 1, sp_passed)
                    sp.dma_start(ein[:, p, :].rearrange("p (c f) -> p c f", f=D),
                                 edge_v[:, bass.ds(g * QUAD, QUAD), :]).then_inc(e_loaded[p], 16)
                elif s < FINAL:
                    wait_alone(sp, e_shifted, EGROUPS * (s - 1) + g - 1, sp_passed)
                    if s <= LAYERS - 1:
                        wait_alone(sp, e_product, H * (EGROUPS * s + g - 1), sp_passed)
                    sp.dma_start(ein[:, p, :],
                                 edge_t[bass.ds(g, 1), :, :].rearrange("o p f -> (o p) f")).then_inc(e_loaded[p], 16)

            def sparse_store(s, k, q):
                g, p, i = number(k, q)
                wait_alone(sp, sums_out, EGROUPS * s + g + 1, sp_passed)
                sp.dma_start(sums_v[:, bass.ds(g * QUAD, QUAD), :], res[:, p, :, :]).then_inc(sums_stored[p], 16)
                if s < LAYERS:
                    wait_alone(sp, e_updated, H * (EGROUPS * s + g + 1), sp_passed)
                    sp.dma_start(edge_t[bass.ds(g, 1), :, :].rearrange("o p f -> (o p) f"),
                                 tout[:, p, :, :].rearrange("p h j -> p (h j)")).then_inc(e_stored[p], 16)

            def dense_load(d, k, q):
                g, p, i = number(k, q)
                wait_alone(sp, turned, NGROUPS * d + g - SLOTS + 1, sp_passed)
                if d == FINAL:
                    wait_alone(sp, ln, ln_read(d, k, q, SLOTS), sp_passed)
                table = x_v if d == 0 else nodes_v
                sp.dma_start(rows[:, q, :, :], table[:, bass.ds(g * QUAD, QUAD), :]).then_inc(rows_loaded[q], 16)

            def input_load(k, q):
                g, p, i = number(k, q)
                wait_alone(sp, ln, ln_read(LAST, k, q, 2), sp_passed)
                sp.dma_start(ein[:, p, :].rearrange("p (t f) -> p t f", f=D),
                             x_v[:, bass.ds(g * QUAD, QUAD), :]).then_inc(x_loaded[p], 16)

            def dense_store(d, k, q):
                g, p, i = number(k, q)
                if d < LAST:
                    wait_alone(sp, rows_out, NGROUPS * d + g + 1, sp_passed)
                else:
                    wait_alone(sp, ln_out, NGROUPS * (d - LAST) + g + 1, sp_passed)
                table = out_v if d == FINAL else nodes_v
                sp.dma_start(table[:, bass.ds(g * QUAD, QUAD), :], res[:, p, :, :]).then_inc(nodes_stored[p], 16)

            for s in range(SPARSE):
                if s > 0:
                    if s <= LAYERS:
                        for p in range(2):
                            sp.wait_ge(e_stored[p], 16 * NS[p] * s)
                sparse_load(s, 0, 0)

                def sparse_step(k, q):
                    sparse_load(s, *ahead(k, q))
                    if not starts(k, q, 1):
                        sparse_store(s, *behind(k, q))

                over_groups(sp, 0, EGROUPS - 1, sparse_step)
                sparse_store(s, *place(EGROUPS - 2))
                sparse_store(s, *place(EGROUPS - 1))
                for p in range(2):
                    sp.wait_ge(sums_stored[p], 16 * NS[p] * (s + 1))
                edges = sums[0:EP, :].rearrange("(h q p) f -> q h p f", h=2, q=CH)
                sp.dma_start(run_last[:, :, :], edges[:, :, P - 1, :]).then_inc(runs_loaded, 16)
                sp.dma_start(run_first[:, :, :], edges[:, :, 0, :]).then_inc(runs_loaded, 16)
                if s > 0:
                    for p in range(2):
                        sp.wait_ge(nodes_stored[p], 16 * ND * s)
                else:
                    for p in range(2):
                        sp.wait_ge(rows_scattered[p], 16 * QUAD * NS[p])
                    sp.dma_start(row_idx[:, :], row_of_v).then_inc(row_idx_loaded, 16)
                for g in range(SLOTS - 1):
                    dense_load(s, *place(g))
                sp.wait_ge(runs_summed, s + 1)
                sp.dma_start(sums[SPAN:SPAN + CHUNKS, :].rearrange("(h q) f -> q h f", h=2),
                             run_sum[:, :, :]).then_inc(runs_stored, 16)

                def dense_step(loads):
                    def run(k, q):
                        if loads:
                            dense_load(s, *ahead(k, q, SLOTS - 1))
                        if s == LAST:
                            input_load(k, q)
                        if not starts(k, q, 2):
                            dense_store(s, *behind(k, q, 2))
                    return run

                over_groups(sp, 0, NGROUPS - SLOTS + 1, dense_step(True))
                over_groups(sp, NGROUPS - SLOTS + 1, NGROUPS, dense_step(False))
                for g in range(NGROUPS - 2, NGROUPS):
                    dense_store(s, *place(g))
                for p in range(2):
                    sp.wait_ge(nodes_stored[p], 16 * ND * (s + 1))

        @block.gpsimd
        def _(pool):
            nc.gpsimd.memset(ones[:, :], 1.0).then_inc(const_made, 1)
            nc.gpsimd.memset(res[:, 0, :, :], 0.0).then_inc(const_made, 1)
            nc.gpsimd.iota(zero_rows[:, :], pattern=[[0, TILES]], base=ZERO, channel_multiplier=1).then_inc(const_made, 1)
            nc.gpsimd.iota(j_i[:, :], pattern=[[P, CHUNKS]], base=0, channel_multiplier=1).then_inc(const_made, 1)
            nc.gpsimd.iota(span_i[:, :], pattern=[[1, CHUNKS]], base=SPAN, channel_multiplier=0).then_inc(const_made, 1)
            pool.wait_ge(const_made, 5)
            nc.gpsimd.affine_select(out=ident[:, :], in_=ones[:, :], compare_op=ALU.is_equal, fill=0.0, base=0,
                                    pattern=[[-1, P]], channel_multiplier=1).then_inc(const_made, 1)
            nc.gpsimd.affine_select(out=sel_last[:, :], in_=ones[:, :], compare_op=ALU.is_equal, fill=0.0,
                                    base=-(P - 1), pattern=[[0, P]], channel_multiplier=1).then_inc(const_made, 1)
            nc.gpsimd.affine_select(out=sel_first[:, :], in_=ones[:, :], compare_op=ALU.is_equal, fill=0.0,
                                    base=0, pattern=[[0, P]], channel_multiplier=1).then_inc(const_made, 1)
            pool.wait_ge(prep, 10)
            for h in range(2):
                nc.gpsimd.affine_select(out=links[:, h, :], in_=links[:, h, :], compare_op=ALU.is_gt, fill=0.0,
                                        base=-CH * h, pattern=[[1, CHUNKS]], channel_multiplier=-1).then_inc(links_made, 1)

            def gather(table, index, to, done):
                nc.gpsimd.indirect_dma_start(
                    out=to, out_offset=None, in_=table,
                    in_offset=bass.IndirectOffsetOnAxis(ap=index, axis=0)).then_inc(done, 16)

            for s in range(SPARSE):
                def scatter(k, q):
                    g, p, i = number(k, q)
                    wait_alone(pool, rows_scattered[p], 16 * QUAD * i, pool_passed)
                    at = bass.ds(g * QUAD, QUAD)
                    nc.gpsimd.tensor_copy(row_stage[:, p, :], row_i[:, at]).then_inc(stage_copied, 1)
                    nc.gpsimd.tensor_copy(node_stage[:, p, :], node_i[:, at]).then_inc(stage_copied, 1)
                    wait_alone(pool, stage_copied, 2 * (g + 1), pool_passed)
                    for c in range(QUAD):
                        nc.gpsimd.indirect_dma_start(
                            out=row_of, out_offset=bass.IndirectOffsetOnAxis(ap=node_stage[:, p, c:c + 1], axis=0),
                            in_=row_stage[:, p, c:c + 1], in_offset=None, bounds_check=NP - 1,
                            oob_is_err=False).then_inc(rows_scattered[p], 16)

                def sparse_step(k, q):
                    sparse_gather(k, q)
                    if s == 0 and not starts(k, q, 2):
                        scatter(*behind(k, q, 2))

                def sparse_gather(k, q):
                    g, p, i = number(k, q)
                    u, v = NS[p] * s + i, NS4[q] * s + k
                    wait_alone(pool, sp_got[q], 16 * QUAD * v, pool_passed)
                    nc.gpsimd.tensor_copy(idx[:, q, :], src_i[:, bass.ds(g * QUAD, QUAD)]).then_inc(idx_staged, 1)
                    wait_alone(pool, idx_staged, (EGROUPS + NGROUPS) * s + g + 1, pool_passed)
                    if s < FINAL:
                        wait_alone(pool, msg_made, EGROUPS * s + g - SLOTS + 1, pool_passed)
                    else:
                        wait_alone(pool, seg_turned, g - SLOTS + 1, pool_passed)
                    for c in range(QUAD):
                        gather(x if s == 0 else nodes, idx[:, q, c:c + 1], got[:, q, c, :], sp_got[q])

                if s > 0:
                    for p in range(2):
                        pool.wait_ge(nodes_stored[p], 16 * ND * s)
                else:
                    pool.wait_ge(prep, 10)
                    pool.wait_ge(tables_stored, 32)
                over_groups(pool, 0, EGROUPS, sparse_step)
                if s == 0:
                    scatter(*place(EGROUPS - 2))
                    scatter(*place(EGROUPS - 1))
                for q in range(SLOTS):
                    pool.wait_ge(sp_got[q], 16 * QUAD * NS4[q] * (s + 1))

                def dense_gather(k, q):
                    g, p, i = number(k, q)
                    u, v = ND * s + i, ND4[q] * s + k
                    wait_alone(pool, dn_got[q], 16 * QUAD * v, pool_passed)
                    nc.gpsimd.tensor_copy(idx[:, q, :], row_idx[:, bass.ds(g * QUAD, QUAD)]).then_inc(idx_staged, 1)
                    wait_alone(pool, idx_staged, (EGROUPS + NGROUPS) * s + EGROUPS + g + 1, pool_passed)
                    if s < FINAL:
                        wait_alone(pool, turned, NGROUPS * s + g - SLOTS + 1, pool_passed)
                    else:
                        wait_alone(pool, ln, ln_read(s, k, q, SLOTS), pool_passed)
                    for t in range(QUAD):
                        gather(sums, idx[:, q, t:t + 1], got[:, q, t, :], dn_got[q])

                pool.wait_ge(row_idx_loaded, 16)
                for p in range(2):
                    pool.wait_ge(sums_stored[p], 16 * NS[p] * (s + 1))
                pool.wait_ge(runs_stored, 16 * (s + 1))
                over_groups(pool, 0, NGROUPS, dense_gather)
                for q in range(SLOTS):
                    pool.wait_ge(dn_got[q], 16 * QUAD * ND4[q] * (s + 1))

        @block.tensor
        def _(pe):
            pe.wait_ge(prep, 1)
            pe.wait_ge(const_made, 8)
            for i, ps in enumerate((ps_in, ps_agg, ps_out)):
                for h in range(2):
                    last = nc.tensor.transpose(ps[:, 0, h * CH:(h + 1) * CH], rawf[:, i, h, :], ident[0:CH, 0:CH])
            last.then_inc(prep_pe, 1)
            pe.wait_ge(prep, 2)
            nc.tensor.matmul(ps_back[:, 0, 0:CHUNKS], sel_last[:, :], dcol[:, :], start=True, stop=True)
            nc.tensor.matmul(ps_back[:, 1, 0:CHUNKS], sel_first[:, :], dcol[:, :], start=True,
                             stop=True).then_inc(prep_pe, 1)
            pe.wait_ge(loaded, 16 * 8)

            def sparse(s):
                def turn_edges(k, q):
                    g, p, i = number(k, q)
                    u, v = NS[p] * s + i, NS4[q] * s + k
                    if s == 0:
                        pe.wait_ge(e_loaded[p], 16 * (u + 1))
                        wait(pe, e_turned_out, H * g)
                        for h in range(H):
                            for c in range(QUAD):
                                last = nc.tensor.transpose(
                                    ps_in[:, h, c * P:(c + 1) * P],
                                    ein[:, p, c * D + h * P:c * D + (h + 1) * P], ident[:, :])
                    else:
                        pe.wait_ge(e_shifted, EGROUPS * (s - 1) + g + 1)
                        wait(pe, msg_summed, EGROUPS * s + g)
                        for c in range(QUAD):
                            for h in range(H):
                                last = nc.tensor.transpose(as_rows(ps_in)[:, c, h * P:(h + 1) * P],
                                                           tin[:, p, h, c * P:(c + 1) * P], ident[:, :])
                    last.then_inc(e_turned, 1)

                def update_edges(k, q):
                    g, p, i = number(k, q)
                    G = EGROUPS * s + g
                    if s == 0:
                        pe.wait_ge(e_turned_out, H * (g + 1))
                    src_t = tin[:, p, :, :] if s == 0 else ein[:, p, :].rearrange("p (h j) -> p h j", h=H)
                    for ho in range(H):
                        wait(pe, e_updated, H * G - H + 1 + ho)
                        for h in range(H):
                            last = nc.tensor.matmul(ps_out[:, ho, :], we[:, s, h, ho * P:(ho + 1) * P], src_t[:, h, :],
                                                    start=(h == 0), stop=(h == H - 1))
                        last.then_inc(e_product, 1)

                def sum_messages(k, q):
                    g, p, i = number(k, q)
                    pe.wait_ge(same_made, EGROUPS * s + g + 1)
                    pe.wait_ge(msg_made, EGROUPS * s + g + 1)
                    wait(pe, sums_out, EGROUPS * s + g)
                    for c in range(QUAD):
                        last = nc.tensor.matmul(as_rows(ps_agg)[:, c, :], same[:, p, c, :], mid[:, p, c, :],
                                                start=True, stop=True)
                    last.then_inc(sums_made, 1)

                def step(k, q):
                    turn_edges(k, q)
                    if s == 0:
                        sum_messages(k, q)
                        update_edges(k, q)
                    else:
                        if s < LAYERS:
                            update_edges(k, q)
                        sum_messages(k, q)

                over_groups(pe, 0, EGROUPS, step)

            def sparse_final():
                s = FINAL

                def sum_turned(k, q):
                    g, p, i = number(k, q)
                    u, v = NS[p] * s + i, NS4[q] * s + k
                    pe.wait_ge(sp_got[q], 16 * QUAD * (v + 1))
                    pe.wait_ge(same_made, EGROUPS * s + g + 1)
                    wait(pe, seg_turned_out, H * g)
                    for c in range(QUAD):
                        for h in range(H):
                            last = nc.tensor.matmul(ps_in[:, h, c * P:(c + 1) * P], got[:, q, c, h * P:(h + 1) * P],
                                                    same[:, p, c, :], start=True, stop=True)
                    last.then_inc(seg_turned, 1)

                def times_m(k, q):
                    g, p, i = number(k, q)
                    pe.wait_ge(seg_turned_out, H * (g + 1))
                    wait(pe, sums_out, EGROUPS * s + g)
                    for c in range(QUAD):
                        for h in range(H):
                            last = nc.tensor.matmul(as_rows(ps_agg)[:, c, :], tin[:, p, h, c * P:(c + 1) * P],
                                                    m1[:, h, :], start=(h == 0), stop=(h == H - 1))
                    last.then_inc(sums_made, 1)

                def step(k, q):
                    sum_turned(k, q)
                    times_m(*behind(k, q))

                sum_turned(0, 0)
                over_groups(pe, 1, EGROUPS, step)
                times_m(*place(EGROUPS - 1))

            def runs(s):
                pe.wait_ge(runs_loaded, 32 * (s + 1))
                pe.wait_ge(links_made, 2)
                pe.wait_ge(sums_out, EGROUPS * (s + 1))
                for ho in range(2):
                    for h in range(2):
                        last = nc.tensor.matmul(ps_agg[0:CH, ho, 0:D], links[:, h, ho * CH:(ho + 1) * CH],
                                                run_last[:, h, :], start=(h == 0), stop=(h == 1))
                last.then_inc(runs_product, 1)
                pe.wait_ge(runs_summed, s + 1)

            def dense(d):
                wl = min(d, LAYERS - 1)

                def turn_in(k, q):
                    g, p, i = number(k, q)
                    u, v = ND * d + i, ND4[q] * d + k
                    pe.wait_ge(rows_loaded[q], 16 * (v + 1))
                    wait(pe, scaled, H * (NGROUPS * d + g))
                    for h in range(H):
                        for t in range(QUAD):
                            last = nc.tensor.transpose(ps_in[:, h, t * P:(t + 1) * P],
                                                       rows[:, q, t, h * P:(h + 1) * P], ident[:, :])
                    if d < FINAL:
                        pe.wait_ge(dn_got[q], 16 * QUAD * (v + 1))
                        wait(pe, added, H * (NGROUPS * d + g))
                        for h in range(H):
                            for t in range(QUAD):
                                last = nc.tensor.transpose(ps_agg[:, h, t * P:(t + 1) * P],
                                                           got[:, q, t, h * P:(h + 1) * P], ident[:, :])
                    last.then_inc(turned, 1)

                def main(k, q):
                    g, p, i = number(k, q)
                    G = NGROUPS * d + g
                    if d < FINAL:
                        pe.wait_ge(added, H * (G + 1))
                        for ho in range(H):
                            wait(pe, activated, H * G - H + 1 + ho)
                            for h in range(H):
                                last = nc.tensor.matmul(ps_out[:, ho, :], wc[:, wl, h, ho * P:(ho + 1) * P],
                                                        tin[:, p, h, :], start=(h == 0), stop=(h == H - 1))
                            last.then_inc(product, 1)
                    else:
                        pe.wait_ge(scaled, H * (G + 1))
                        wait(pe, ln, ln_read(d, k, q, 2) - 1)
                        for t in range(QUAD):
                            for h in range(H):
                                last = nc.tensor.matmul(as_rows(ps_final[p])[:, t, :], tin[:, p, h, t * P:(t + 1) * P],
                                                        w1[:, h, :], start=(h == 0), stop=(h == H - 1))
                        last.then_inc(product, 1)

                def turn_back(k, q):
                    g, p, i = number(k, q)
                    pe.wait_ge(activated, H * (NGROUPS * d + g + 1))
                    if d < LAST:
                        wait(pe, rows_out, NGROUPS * d + g)
                    else:
                        wait(pe, ln, ln_read(d, k, q, 1))
                    for t in range(QUAD):
                        for h in range(H):
                            last = nc.tensor.transpose(as_rows(ps_back)[:, t, h * P:(h + 1) * P],
                                                       tout[:, p, h, t * P:(t + 1) * P], ident[:, :])
                    last.then_inc(back, 1)

                def step(k, q):
                    turn_in(*ahead(k, q))
                    main(k, q)
                    if d < FINAL and not starts(k, q, 1):
                        turn_back(*behind(k, q))

                end = NGROUPS - 1
                turn_in(0, 0)
                over_groups(pe, 0, end, step)
                main(*place(end))
                if d < FINAL:
                    turn_back(*place(end - 1))
                    turn_back(*place(end))

            for s in range(SPARSE):
                sparse_final() if s == FINAL else sparse(s)
                runs(s)
                dense(s)
                if s < LAYERS:
                    pe.wait_ge(bn, BN_STEPS * (s + 1))
                    for h in range(H):
                        last = nc.tensor.matmul(ps_back[:, 0, h * P:(h + 1) * P], ones[:, :], diag[:, h, :],
                                                start=True, stop=True)
                    last.then_inc(bn_row, 1)
                    pe.wait_ge(bn_row_out, s + 1)

        @block.scalar
        def _(act):
            def sparse(s):
                def step(k, q):
                    g, p, i = number(k, q)
                    u, v = NS[p] * s + i, NS4[q] * s + k
                    G = EGROUPS * s + g

                    def messages():
                        act.wait_ge(msg_summed, G + 1)
                        wait(act, sums_made, G - 1)
                        nc.scalar.activation(mid[:, p, :, :], got[:, q, :, :], ACT.Relu).then_inc(msg_made, 1)

                    def updates():
                        for ho in range(H):
                            act.wait_ge(e_product, H * G + ho + 1)
                            wait(act, e_stored[p], 16 * u)
                            nc.scalar.activation(tout[:, p, ho, :], ps_out[:, ho, :], ACT.Relu,
                                                 bias=be[:, s, ho:ho + 1]).then_inc(e_updated, 1)

                    def results():
                        act.wait_ge(sums_made, G + 1)
                        wait(act, sums_stored[p], 16 * u)
                        nc.scalar.copy(res[:, p, :, :], as_rows(ps_agg)).then_inc(sums_out, 1)

                    if s == FINAL:
                        results()
                        return
                    if s == 0:
                        for h in range(H):
                            act.wait_ge(e_turned, G + 1)
                            wait(act, e_product, H * (G - 1))
                            nc.scalar.copy(tin[:, p, h, :], ps_in[:, h, :]).then_inc(e_turned_out, 1)
                        messages()
                        results()
                        updates()
                    else:
                        messages()
                        if s < LAYERS:
                            updates()
                        results()

                def turned_sums(k, q):
                    g, p, i = number(k, q)
                    for h in range(H):
                        act.wait_ge(seg_turned, g + 1)
                        wait(act, sums_made, EGROUPS * s + g - 1)
                        nc.scalar.copy(tin[:, p, h, :], ps_in[:, h, :]).then_inc(seg_turned_out, 1)

                def final_step(k, q):
                    turned_sums(k, q)
                    step(*behind(k, q))

                if s == FINAL:
                    turned_sums(0, 0)
                    over_groups(act, 1, EGROUPS, final_step)
                    step(*place(EGROUPS - 1))
                else:
                    over_groups(act, 0, EGROUPS, step)

            def dense(d):
                wl = min(d, LAYERS - 1)

                def scale_in(k, q):
                    g, p, i = number(k, q)
                    G = NGROUPS * d + g
                    act.wait_ge(turned, G + 1)
                    for h in range(H):
                        if d == FINAL:
                            wait(act, product, H * NGROUPS * FINAL + g - 1)
                            nc.scalar.copy(tin[:, p, h, :], ps_in[:, h, :]).then_inc(scaled, 1)
                        else:
                            wait(act, product, H * (G - 1))
                            nc.scalar.activation(tin[:, p, h, :], ps_in[:, h, :], ACT.Identity,
                                                 bias=shift[:, h:h + 1], scale=scale[:, h:h + 1]).then_inc(scaled, 1)

                def activate(k, q):
                    g, p, i = number(k, q)
                    G = NGROUPS * d + g
                    for ho in range(H):
                        act.wait_ge(product, H * G + ho + 1)
                        if not starts(k, q, 2):
                            wait(act, back, G - 1)
                            if d < LAYERS:
                                wait(act, counted, H * (G - 1))
                        nc.scalar.activation(tout[:, p, ho, :], ps_out[:, ho, :], ACT.Relu,
                                             bias=bc[:, wl, ho:ho + 1]).then_inc(activated, 1)

                def deviations(k, q):
                    g, p, i = number(k, q)
                    g = NGROUPS * (d - LAST) + g
                    act.wait_ge(ln, LN_STEPS * (g + 1))
                    nc.scalar.activation(ln_std[:, p, :], ln_mv[:, p, :, 1], ACT.Sqrt, bias=eps[:, 0:1]).then_inc(
                        ln_std_made, 1)

                def step(k, q):
                    scale_in(*ahead(k, q))
                    if d == LAST and not starts(k, q, 2):
                        deviations(*behind(k, q, 2))
                    if d == FINAL and not starts(k, q, 1):
                        deviations(*behind(k, q))
                    if d < FINAL:
                        activate(k, q)

                end = NGROUPS - 1
                if d == 0:
                    act.wait_ge(prep, 13)
                elif d < FINAL:
                    act.wait_ge(bn, BN_STEPS * min(d, LAYERS))
                scale_in(0, 0)
                over_groups(act, 0, end, step)
                if d < FINAL:
                    activate(*place(end))
                if d >= LAST:
                    for g in range(end - (2 if d == LAST else 1), end + 1):
                        deviations(*place(g))

            act.wait_ge(loaded, 16 * 8)
            for s in range(SPARSE):
                if 0 < s < LAYERS:
                    act.wait_ge(back, NGROUPS * s)
                    act.wait_ge(counted, H * NGROUPS * s)
                sparse(s)
                if s < LAYERS:
                    for p in range(2):
                        act.wait_ge(e_stored[p], 16 * NS[p] * (s + 1))
                dense(s)
                if s < LAYERS:
                    act.wait_ge(bn, BN_STEPS * s + 1)
                    nc.scalar.activation(bn_std[:, :], mv[:, :, 1], ACT.Sqrt, bias=eps[:, 0:1]).then_inc(bn_std_made, 1)
                    act.wait_ge(bn_row, s + 1)
                    nc.scalar.copy(scale_row[:, :], ps_back[:, 0, 0:D]).then_inc(bn_row_out, 1)

        @block.vector
        def _(dve):
            dve.wait_ge(raw_loaded, 48)
            nc.vector.tensor_copy(rawf[:, :, :, :], raw[:, :, :, :]).then_inc(prep, 1)
            dve.wait_ge(prep_pe, 1)
            nc.vector.tensor_copy(dcol[:, :], ps_in[:, 0, 0:CHUNKS]).then_inc(prep, 1)
            nc.vector.tensor_copy(src_i[:, :], ps_out[:, 0, 0:CHUNKS]).then_inc(prep, 1)
            nc.vector.tensor_copy(dnext[:, :], ps_agg[:, 0, 0:CHUNKS]).then_inc(prep, 1)
            nc.vector.memset(prev_last[:, 0:1], -1.0).then_inc(prep, 1)
            dve.wait_ge(prep_pe, 2)
            nc.vector.tensor_copy(prev_last[:, 1:CHUNKS], ps_back[:, 0, 0:CHUNKS - 1]).then_inc(prep, 1)
            nc.vector.tensor_copy(first_row[:, :], ps_back[0:CH, 1, 0:CHUNKS]).then_inc(prep, 1)
            dve.wait_ge(const_made, 8)
            nc.vector.tensor_copy(j_f[:, :], j_i[:, :]).then_inc(prep, 1)
            dve.wait_ge(prep, 8)
            nc.vector.tensor_tensor(flag[:, :], prev_last[:, :], dcol[:, :], ALU.is_equal).then_inc(steps, 1)
            nc.vector.tensor_tensor(span_f[:, :], span_i[:, :], j_f[:, :], ALU.subtract).then_inc(steps, 1)
            dve.wait_ge(steps, 2)
            nc.vector.tensor_tensor(span_f[:, :], span_f[:, :], flag[:, :], ALU.mult).then_inc(steps, 1)
            dve.wait_ge(steps, 3)
            nc.vector.tensor_tensor(row_i[:, :], span_f[:, :], j_f[:, :], ALU.add).then_inc(steps, 1)
            nc.vector.tensor_tensor(flag[:, :], dnext[:, :], dcol[:, :], ALU.is_equal).then_inc(steps, 1)
            dve.wait_ge(steps, 5)
            nc.vector.scalar_tensor_tensor(out=node_i[:, :], in0=flag[:, :], scalar=float(PAD_DST), in1=dcol[:, :],
                                           op0=ALU.mult, op1=ALU.add).then_inc(steps, 1)
            nc.vector.tensor_scalar(links[:, 0, :], first_row[:, :], rawf[:, 0, 0, P - 1:P], None, ALU.is_equal).then_inc(steps, 1)
            nc.vector.tensor_scalar(links[:, 1, :], first_row[:, :], rawf[:, 0, 1, P - 1:P], None, ALU.is_equal).then_inc(steps, 1)
            dve.wait_ge(steps, 8)
            nc.vector.memset(tmp[:, :], 0.0).then_inc(prep, 1)
            nc.vector.memset(mv[:, :, :], 0.0).then_inc(prep, 1)
            nc.vector.memset(scale[:, :], 1.0).then_inc(prep, 1)
            nc.vector.memset(shift[:, :], 0.0).then_inc(prep, 1)
            nc.vector.memset(eps[:, :], EPS).then_inc(prep, 1)
            dve.wait_ge(loaded, 16 * 8)
            dve.wait_ge(prep, 13)

            def sparse(s):
                def find_same(k, q):
                    g, p, i = number(k, q)
                    u, v = NS[p] * s + i, NS4[q] * s + k
                    if s < FINAL:
                        wait(dve, sums_made, EGROUPS * s + g - 1)
                    else:
                        wait(dve, seg_turned, g - 1)
                    kept = same_all[:, bass.ds(g * QUAD, QUAD), :]
                    if s > 0:
                        nc.vector.tensor_copy(same[:, p, :, :], kept).then_inc(same_made, 1)
                        return
                    dve.wait_ge(drow_loaded[p], 16 * (u + 1))
                    nc.vector.tensor_tensor(
                        same[:, p, :, :], drow[:, p, :].rearrange("p (c j) -> p c j", c=QUAD),
                        dcol[:, bass.ds(g * QUAD, QUAD)].unsqueeze(2).to_broadcast([P, QUAD, P]),
                        ALU.is_equal).then_inc(same_made, 1)
                    dve.wait_ge(same_made, g + 1)
                    nc.vector.tensor_copy(kept, same[:, p, :, :]).then_inc(same_kept, 1)

                def shift_edges(k, q):
                    g, p, i = number(k, q)
                    u, v = NS[p] * s + i, NS4[q] * s + k
                    dve.wait_ge(e_loaded[p], 16 * (u + 1))
                    wait(dve, e_turned, EGROUPS * s + g - 1)
                    for h in range(H):
                        last = nc.vector.tensor_scalar(tin[:, p, h, :], ein[:, p, h * QUAD * P:(h + 1) * QUAD * P],
                                                       shift[:, h:h + 1], None, ALU.add)
                    last.then_inc(e_shifted, 1)

                def messages(k, q):
                    g, p, i = number(k, q)
                    u, v = NS[p] * s + i, NS4[q] * s + k
                    G = EGROUPS * s + g
                    dve.wait_ge(sp_got[q], 16 * QUAD * (v + 1))
                    if s == 0:
                        dve.wait_ge(e_loaded[p], 16 * (u + 1))
                        nc.vector.tensor_tensor(got[:, q, :, :], got[:, q, :, :],
                                                ein[:, p, :].rearrange("p (c f) -> p c f", f=D),
                                                ALU.add).then_inc(msg_summed, 1)
                        return
                    nc.vector.tensor_tensor(got[:, q, :, :], got[:, q, :, :],
                                            scale_row[:, :].unsqueeze(1).to_broadcast([P, QUAD, D]),
                                            ALU.mult).then_inc(got_scaled, 1)
                    dve.wait_ge(got_scaled, G - EGROUPS + 1)
                    dve.wait_ge(e_turned, G + 1)
                    nc.vector.tensor_tensor(got[:, q, :, :], as_rows(ps_in), got[:, q, :, :],
                                            ALU.add).then_inc(msg_summed, 1)

                def step(k, q):
                    if s < FINAL:
                        messages(k, q)
                    if 0 < s < FINAL:
                        shift_edges(*ahead(k, q))
                    find_same(*ahead(k, q))

                if s > 0:
                    dve.wait_ge(same_kept, EGROUPS)
                if 0 < s < FINAL:
                    dve.wait_ge(bn_row_out, s if s < LAYERS else LAYERS)
                    shift_edges(0, 0)
                find_same(0, 0)
                end = EGROUPS - 1
                over_groups(dve, 0, end, step)
                if s < FINAL:
                    messages(*place(end))

            def runs(s):
                dve.wait_ge(runs_product, s + 1)
                dve.wait_ge(runs_loaded, 32 * (s + 1))
                if s > 0:
                    dve.wait_ge(runs_stored, 16 * s)
                nc.vector.tensor_tensor(run_sum[:, :, :], ps_agg[0:CH, :, 0:D], run_first[:, :, :],
                                        ALU.add).then_inc(runs_summed, 1)

            def ln_variance(d, k, q):
                p = q % 2
                done = ln_read(d, k, q)
                dve.wait_ge(ln, done)
                for t in range(QUAD):
                    last = nc.vector.bn_stats(ln_stats[:, p, t, :], mid[:, p, t, :])
                last.then_inc(ln, 1)
                wait_alone(dve, ln, done + 1, dve_passed)
                for t in range(QUAD):
                    last = nc.vector.bn_aggr(ln_mv[:, p, t, :], ln_stats[:, p, t, :])
                last.then_inc(ln, 1)

            def ln_rows(d, k, q):
                g, p, i = number(k, q)
                g = NGROUPS * (d - LAST) + g
                dve.wait_ge(ln_std_made, g + 1)
                nc.vector.reciprocal(ln_rstd[:, p, :], ln_std[:, p, :]).then_inc(ln_rstd_made, 1)
                dve.wait_ge(ln_rstd_made, g + 1)
                wait(dve, nodes_stored[p], 16 * (ND * d + i))
                for t in range(QUAD):
                    last = nc.vector.tensor_scalar(res[:, p, t, :], mid[:, p, t, :], ln_mv[:, p, t, 0:1],
                                                   ln_rstd[:, p, t:t + 1], ALU.subtract, ALU.mult)
                last.then_inc(ln_out, 1)

            def dense(d):
                def add_sums(k, q):
                    g, p, i = number(k, q)
                    G = NGROUPS * d + g
                    for h in range(H):
                        dve.wait_ge(scaled, H * G + h + 1)
                        nc.vector.tensor_tensor(tin[:, p, h, :], ps_agg[:, h, :], tin[:, p, h, :],
                                                ALU.add).then_inc(added, 1)

                def count(k, q, full):
                    g, p, i = number(k, q)
                    G = NGROUPS * d + g
                    for h in range(H):
                        dve.wait_ge(activated, H * G + h + 1)
                        to = stats[:, h, bass.ds(g, 1), :].rearrange("p o s -> p (o s)")
                        if full:
                            of = tout[:, p, h, :]
                        else:
                            of = tout[:, p, h, :].rearrange("p (t j) -> p t j", j=P)[:, :, 0:P - 1]
                        nc.vector.bn_stats(to, of).then_inc(counted, 1)

                def copy_rows(k, q):
                    g, p, i = number(k, q)
                    u, v = ND * d + i, ND4[q] * d + k
                    dve.wait_ge(back, NGROUPS * d + g + 1)
                    wait(dve, nodes_stored[p], 16 * u)
                    nc.vector.tensor_copy(res[:, p, :, :], as_rows(ps_back)).then_inc(rows_out, 1)

                def last_conv_rows(k, q):
                    g, p, i = number(k, q)
                    wait(dve, ln_out, NGROUPS * (d - LAST) + g - 1)
                    dve.wait_ge(x_loaded[p], 16 * (i + 1))
                    dve.wait_ge(back, NGROUPS * d + g + 1)
                    nc.vector.scalar_tensor_tensor(
                        out=mid[:, p, :, :], in0=ein[:, p, :].rearrange("p (t f) -> p t f", f=D), scalar=2.0,
                        in1=as_rows(ps_back), op0=ALU.mult, op1=ALU.add).then_inc(ln, 2)
                    ln_variance(d, k, q)

                def final_rows(k, q):
                    g, p, i = number(k, q)
                    u, v = ND * d + i, ND4[q] * d + k
                    wait(dve, ln_out, NGROUPS * (d - LAST) + g - 1)
                    dve.wait_ge(dn_got[q], 16 * QUAD * (v + 1))
                    dve.wait_ge(product, H * NGROUPS * FINAL + g + 1)
                    nc.vector.tensor_tensor(mid[:, p, :, :], as_rows(ps_final[p]), got[:, q, :, :],
                                            ALU.add).then_inc(ln, 1)
                    dve.wait_ge(ln, ln_read(d, k, q) - 1)
                    nc.vector.scalar_tensor_tensor(out=mid[:, p, :, :], in0=mid[:, p, :, :], scalar=0.0,
                                                   in1=rows[:, q, :, :], op0=ALU.max, op1=ALU.add).then_inc(ln, 1)
                    ln_variance(d, k, q)
                    if not starts(k, q, 1):
                        ln_rows(d, *behind(k, q))

                def step(full):
                    def run(k, q):
                        add_sums(*ahead(k, q))
                        if d < LAYERS:
                            count(k, q, full)
                        if d == LAST and not starts(k, q, 2):
                            ln_rows(d, *behind(k, q, 2))
                        if not starts(k, q, 1):
                            (copy_rows if d < LAST else last_conv_rows)(*behind(k, q))
                    return run

                end = NGROUPS - 1
                if d == FINAL:
                    over_groups(dve, 0, NGROUPS, final_rows)
                    ln_rows(d, *place(end))
                    return
                add_sums(0, 0)
                over_groups(dve, 0, FULL, step(True))
                over_groups(dve, FULL, end, step(False))
                if d < LAYERS:
                    count(*place(end), False)
                for g in (end - 1, end):
                    if d == LAST:
                        ln_rows(d, *place(g - 1))
                    (copy_rows if d < LAST else last_conv_rows)(*place(g))
                if d == LAST:
                    ln_rows(d, *place(end))

            def batch_norm(d):
                done = BN_STEPS * d
                dve.wait_ge(counted, H * NGROUPS * (d + 1))
                for h in range(H):
                    last = nc.vector.bn_aggr(mv[:, h, :], stats[:, h, :, :].rearrange("p g s -> p (g s)"))
                last.then_inc(bn, 1)
                dve.wait_ge(bn, done + 1)
                dve.wait_ge(bn_std_made, d + 1)
                nc.vector.reciprocal(rstd[:, :], bn_std[:, :]).then_inc(bn, 1)
                dve.wait_ge(bn, done + 2)
                nc.vector.tensor_tensor(scale[:, :], rstd[:, :], gam[:, d, :], ALU.mult).then_inc(bn, 1)
                dve.wait_ge(bn, done + 3)
                nc.vector.tensor_tensor(tmp[:, :], mv[:, :, 0], scale[:, :], ALU.mult).then_inc(bn, 1)
                for h in range(H):
                    last = nc.vector.tensor_scalar(diag[:, h, :], ident[:, :], scale[:, h:h + 1], None, ALU.mult)
                last.then_inc(bn, 1)
                dve.wait_ge(bn, done + 5)
                nc.vector.tensor_tensor(shift[:, :], bet[:, d, :], tmp[:, :], ALU.subtract).then_inc(bn, 1)
                dve.wait_ge(bn, done + 6)

            for s in range(SPARSE):
                sparse(s)
                runs(s)
                dense(s)
                if s < LAYERS:
                    batch_norm(s)


def kernel(x, src, dst, edge_attr_256, L0_gnn_W_conv, L0_gnn_b_conv, L0_gnn_W_edge, L0_gnn_b_edge, L0_gnn_gamma,
           L0_gnn_beta, L1_gnn_W, L1_gnn_M):
    import numpy as np
    import concourse.bacc as bacc
    from concourse.bass_utils import run_bass_kernel_spmd

    def pad(a, rows, value=0):
        a = np.asarray(a)
        return np.concatenate([a, np.full((rows - a.shape[0],) + a.shape[1:], value, a.dtype)])

    def halves(w):
        w = np.asarray(w)
        lead = w.shape[:-2]
        w = w.reshape(lead + (H, P, w.shape[-1]))
        return np.ascontiguousarray(np.moveaxis(w, -2, 0))

    def columns(b):
        b = np.asarray(b)
        return np.ascontiguousarray(np.moveaxis(b.reshape(b.shape[0], H, P), -1, 0))

    dst_padded = pad(pad(dst, EP, PAD_DST), EP + 1, END_DST)
    arrays = {
        "x": pad(x, NP), "src": pad(src, EP), "dst": dst_padded, "edge": pad(edge_attr_256, EP),
        "w_conv": halves(L0_gnn_W_conv), "b_conv": columns(L0_gnn_b_conv), "w_edge": halves(L0_gnn_W_edge),
        "b_edge": columns(L0_gnn_b_edge), "gamma": columns(L0_gnn_gamma), "beta": columns(L0_gnn_beta),
        "l1_w": halves(L1_gnn_W), "l1_m": halves(L1_gnn_M),
    }
    nc = bacc.Bacc("TRN2", target_bir_lowering=False, num_devices=1)
    feeds, args = {}, {}
    for name, a in arrays.items():
        feeds[f"in_{name}"] = a
        args[name] = nc.dram_tensor(f"in_{name}", a.shape, mybir.dt.from_np(a.dtype), kind="ExternalInput").ap()
    out = nc.dram_tensor("out_nodes", (NP, D), F32, kind="ExternalOutput").ap()
    gnn_kernel(nc, **args, out=out)
    got = run_bass_kernel_spmd(nc, [feeds], core_ids=[0])
    return got.results[0]["out_nodes"][0:N]
```

```python
from contextlib import ExitStack

import concourse.bass as bass
from concourse import mybir

ALU = mybir.AluOpType
ACT = mybir.ActivationFunctionType
F32 = mybir.dt.float32
F32R = mybir.dt.float32r
I32 = mybir.dt.int32
U8 = mybir.dt.uint8

P = 128
D = 256
H = D // P
QUAD = 4
SLOTS = 4
N = 50000
E = 25000
LAYERS = 4
EPS = 1e-5

CHUNKS = -(-E // P)
EP = CHUNKS * P
EGROUPS = CHUNKS // QUAD
CH = CHUNKS // 2
NGROUPS = -(-N // (P * QUAD))
TILES = NGROUPS * QUAD
NP = TILES * P
FULL = (N - (P - 1) * TILES) // QUAD
PAD_DST = 1 << 20
END_DST = 1 << 21
SPAN = EP
ZERO = SPAN + CHUNKS
SUMS = ZERO + P
BLOCKS = 7
BLOCK = EP // BLOCKS
assert EP % BLOCKS == 0 and BLOCK <= SLOTS * QUAD * D
assert CHUNKS % QUAD == 0 and (N - (P - 1) * TILES) % QUAD == 0


def over_groups(eng, first, last, step):
    g = first
    while g < last and (g < SLOTS or g % SLOTS):
        step(*place(g))
        g += 1
    rounds = (last - g) // SLOTS
    if rounds > 0:
        with eng.Fori(g // SLOTS, g // SLOTS + rounds) as k:
            for q in range(SLOTS):
                step(k, q)
        g += SLOTS * rounds
    while g < last:
        step(*place(g))
        g += 1


def place(g):
    return g // SLOTS, g % SLOTS


def ahead(k, q, by=1):
    turn, q = (q + by) // SLOTS, (q + by) % SLOTS
    return (k + turn if turn > 0 else k - -turn if turn < 0 else k), q


def behind(k, q, by=1):
    return ahead(k, q, -by)


def number(k, q):
    return SLOTS * k + q, q % 2, SLOTS // 2 * k + q // 2


def starts(k, q, groups):
    return isinstance(k, int) and SLOTS * k + q < groups


def wait(eng, sem, value):
    if not isinstance(value, int) or value > 0:
        eng.wait_ge(sem, value)


def wait_alone(eng, sem, value, passed):
    wait(eng, sem, value)
    if not isinstance(value, int):
        eng.sem_inc(passed, 1)


def gnn_kernel(nc, x, src, dst, edge, w_conv, b_conv, w_edge, b_edge, gamma, beta, l1_w, l1_m, out):
    ctx = ExitStack()
    with ctx:
        def sb(name, shape, dt=F32):
            return ctx.enter_context(nc.sbuf_tensor(name, shape, dt))

        def sem(name):
            return ctx.enter_context(nc.semaphore(name))

        def slots(name, n=2):
            return [sem(f"{name}{i}") for i in range(n)]

        nodes = nc.dram_tensor("nodes", [NP, D], F32).ap()
        sums = nc.dram_tensor("sums", [SUMS, D], F32).ap()
        edge_t = nc.dram_tensor("edge_t", [EGROUPS, P, H * QUAD * P], F32).ap()
        dst_sorted = nc.dram_tensor("dst_sorted", [EP + 1, 1], I32).ap()
        src_sorted = nc.dram_tensor("src_sorted", [EP, 1], I32).ap()
        edge_sorted = nc.dram_tensor("edge_sorted", [EP, D], F32).ap()
        row_of = nc.dram_tensor("row_of", [NP, 1], I32).ap()

        def tiles(ap):
            return ap.rearrange("(p t) f -> p t f", p=P)

        nodes_v, x_v, out_v = tiles(nodes), tiles(x), tiles(out)
        row_of_v = row_of.rearrange("(p t) o -> p (t o)", p=P)
        sums_v = sums[0:EP, :].rearrange("(c p) f -> p c f", p=P)
        edge_v, edge_sorted_v = (a.rearrange("(c p) f -> p c f", p=P) for a in (edge, edge_sorted))

        def chunk_rows(ap):
            return ap.rearrange("(h q p) -> q h p", h=2, q=CH)

        wc = sb("wc", [P, LAYERS, H, D])
        we = sb("we", [P, LAYERS, H, D])
        we_high, we_low = sb("we_high", [P, H, D], F32R), sb("we_low", [P, H, D], F32R)
        wc_high, wc_low = sb("wc_high", [P, H, D], F32R), sb("wc_low", [P, H, D], F32R)
        w1 = sb("w1", [P, H, D])
        m1 = sb("m1", [P, H, D])
        bc = sb("bc", [P, LAYERS, H])
        be = sb("be", [P, LAYERS, H])
        gam = sb("gam", [P, LAYERS, H])
        bet = sb("bet", [P, LAYERS, H])
        ones = sb("ones", [P, P])
        ident = sb("ident", [P, P])
        sel_last = sb("sel_last", [P, P])
        sel_first = sb("sel_first", [P, P])

        raw = sb("raw", [CH, 3, 2, P], I32)
        rawf = sb("rawf", [CH, 3, 2, P])
        dcol = sb("dcol", [P, CHUNKS])
        dnext = sb("dnext", [P, CHUNKS])
        src_i = sb("src_i", [P, CHUNKS], I32)
        prev_last = sb("prev_last", [P, CHUNKS])
        first_row = sb("first_row", [CH, CHUNKS])
        links = sb("links", [CH, 2, CHUNKS])
        j_i = sb("j_i", [P, CHUNKS], I32)
        span_i = sb("span_i", [P, CHUNKS], I32)
        j_f = sb("j_f", [P, CHUNKS])
        span_f = sb("span_f", [P, CHUNKS])
        flag = sb("flag", [P, CHUNKS])
        row_i = sb("row_i", [P, CHUNKS], I32)
        node_i = sb("node_i", [P, CHUNKS], I32)
        zero_rows = sb("zero_rows", [P, TILES], I32)
        row_stage = sb("row_stage", [P, 2, QUAD], I32)
        node_stage = sb("node_stage", [P, 2, QUAD], I32)

        bad = sb("bad", [CH, 2, P])
        bad_any = sb("bad_any", [CH, 1])
        unsorted_i = sb("unsorted_i", [P, 1], I32)
        column = sb("column", [P, 2])
        before_count = sb("before_count", [P, 1])
        rank_stage = sb("rank_stage", [P, 1], I32)
        dst_stage = sb("dst_stage", [P, 1], I32)
        src_stage = sb("src_stage", [P, 1], I32)

        stats = sb("stats", [P, H, NGROUPS, 6])
        mv = sb("mv", [P, H, 2])
        rstd = sb("rstd", [P, H])
        scale = sb("scale", [P, H])
        shift = sb("shift", [P, H])
        tmp = sb("tmp", [P, H])
        diag = sb("diag", [P, H, P])
        scale_row = sb("scale_row", [P, D])

        idx = sb("idx", [P, SLOTS, QUAD], I32)
        row_idx = sb("row_idx", [P, TILES], I32)
        got = sb("got", [P, SLOTS, QUAD, D])
        ein = sb("ein", [P, SLOTS, QUAD * D])
        rows = sb("rows", [P, SLOTS, QUAD, D])
        tin = sb("tin", [P, 2, H, QUAD * P])
        tin_high = sb("tin_high", [P, 2, H, QUAD * P], F32R)
        tin_low = sb("tin_low", [P, 2, H, QUAD * P], F32R)
        tout = sb("tout", [P, 2, H, QUAD * P])
        mid = sb("mid", [P, 2, QUAD, D])
        res = sb("res", [P, 2, QUAD, D])
        drow = sb("drow", [P, 2, QUAD * P], I32)
        same = sb("same", [P, 2, QUAD, P])
        same_all = sb("same_all", [P, CHUNKS, P], U8)
        ln_stats = sb("ln_stats", [P, 2, QUAD, 6])
        ln_mv = sb("ln_mv", [P, 2, QUAD, 2])
        ln_std = sb("ln_std", [P, 2, QUAD])
        eps = sb("eps", [P, 1])
        bn_std = sb("bn_std", [P, H])
        ln_rstd = sb("ln_rstd", [P, 2, QUAD])
        ln_bias = sb("ln_bias", [P, 2, QUAD])
        run_last = sb("run_last", [CH, 2, D])
        run_first = sb("run_first", [CH, 2, D])
        run_sum = sb("run_sum", [CH, 2, D])

        def ln_input(d, q):
            if d < FINAL or q < 2:
                return mid[:, q % 2, :, :]
            return tout[:, q - 2, :, :].rearrange("p h (k f) -> p (h k) f", f=D)

        def bank2(name):
            return ctx.enter_context(nc.psum_tensor(name, [P, H, QUAD * P], F32))

        ps_in, ps_agg, ps_out, ps_back = (bank2(n) for n in ("ps_in", "ps_agg", "ps_out", "ps_back"))

        ps_final = ps_out, ps_back
        ps_rows = ps_in, ps_agg
        ps_edges = ps_in, ps_back

        def as_rows(ps):
            return ps[:, :, :].rearrange("p h (k f) -> p (h k) f", f=D)

        def flat(buf, dt=F32):
            ap = buf[:, :, :, :].rearrange("p s c f -> p (s c f)")
            return (ap if dt == F32 else ap.bitcast(dt))[:, 0:BLOCK]

        block_i = ein[:, :, :].rearrange("p s f -> p (s f)").bitcast(I32)[:, 0:BLOCK]
        block_less = ein[:, :, :].rearrange("p s f -> p (s f)")[:, 0:BLOCK]
        block_dst, place_i, block_earlier = flat(got), flat(rows, I32), flat(rows)
        places = same_all[:, :, :].rearrange("p c j -> p (c j)").bitcast(F32)[:, 0:BLOCK]
        counts = mid[:, :, :, :].rearrange("p s c f -> p (s c f)")[:, 0:BLOCKS * CHUNKS].rearrange(
            "p (b c) -> p b c", b=BLOCKS)

        loaded = sem("loaded")
        raw_loaded = sem("raw_loaded")
        const_made = sem("const_made")
        prep = sem("prep")
        prep_pe = sem("prep_pe")
        links_made = sem("links_made")
        tables_stored = sem("tables_stored")
        stage_copied = sem("stage_copied")
        row_idx_loaded = sem("row_idx_loaded")
        idx_staged = sem("idx_staged")
        rows_scattered = slots("rows_scattered")

        order = sem("order")
        order_pe = sem("order_pe")
        order_known = sem("order_known")
        columns_loaded = sem("columns_loaded")
        places_made = sem("places_made")
        block_loaded = sem("block_loaded")
        block_used = sem("block_used")
        ranking = sem("ranking")
        ranks_made = sem("ranks_made")
        rank_staged = sem("rank_staged")
        chunk_loaded = sem("chunk_loaded")
        chunk_scattered = sem("chunk_scattered")
        end_stored = sem("end_stored")
        raw_reloaded = sem("raw_reloaded")

        sp_got = slots("sp_got", SLOTS)
        e_loaded, drow_loaded = slots("e_loaded", SLOTS), slots("drow_loaded")
        e_shifted = sem("e_shifted")
        same_made = sem("same_made")
        same_kept = sem("same_kept")
        got_scaled = sem("got_scaled")
        msg_summed = sem("msg_summed")
        weights_split = sem("weights_split")
        e_high = sem("e_high")
        e_split = sem("e_split")
        seg_split = sem("seg_split")
        rows_turned = sem("rows_turned")
        z_high = sem("z_high")
        z_split = sem("z_split")
        msg_made = sem("msg_made")
        e_turned = sem("e_turned")
        e_product = sem("e_product")
        e_updated = sem("e_updated")
        sums_made = sem("sums_made")
        sums_out = sem("sums_out")
        sums_stored, e_stored = map(slots, ("sums_stored", "e_stored"))
        seg_turned = sem("seg_turned")
        seg_turned_out = sem("seg_turned_out")
        runs_loaded = sem("runs_loaded")
        runs_product = sem("runs_product")
        runs_summed = sem("runs_summed")
        runs_stored = sem("runs_stored")

        rows_loaded, dn_got = slots("rows_loaded", SLOTS), slots("dn_got", SLOTS)
        nodes_stored, x_loaded = slots("nodes_stored"), slots("x_loaded")
        turned = sem("turned")
        scaled = sem("scaled")
        added = sem("added")
        product = sem("product")
        activated = sem("activated")
        counted = sem("counted")
        back = sem("back")
        rows_out = sem("rows_out")
        ln = sem("ln")
        bn = sem("bn")
        bn_row = sem("bn_row")
        bn_row_out = sem("bn_row_out")
        ln_rstd_made = sem("ln_rstd_made")
        ln_std_made = sem("ln_std_made")
        ln_factored = sem("ln_factored")
        ln_out = sem("ln_out")
        sp_passed, pool_passed, dve_passed = sem("sp_passed"), sem("pool_passed"), sem("dve_passed")
        bn_std_made = sem("bn_std_made")
        steps = sem("row_steps")

        NS = (EGROUPS + 1) // 2, EGROUPS // 2
        ND = NGROUPS // 2
        NS4 = [len(range(q, EGROUPS, SLOTS)) for q in range(SLOTS)]
        ND4 = [len(range(q, NGROUPS, SLOTS)) for q in range(SLOTS)]
        SPARSE = LAYERS + 2
        LAST = LAYERS
        FINAL = LAYERS + 1

        BN_STEPS = 6
        LN_STEPS = 4

        def ln_read(d, k, q, ago=0):
            return LN_STEPS * (NGROUPS * (d - LAST) + SLOTS * k + q - ago) + 2

        def three_products(out, ops, start, stop):
            (lh, ll), (rh, rl) = ops
            nc.tensor.matmul(out, lh, rh, start=start, stop=False)
            nc.tensor.matmul(out, lh, rl, start=False, stop=False)
            return nc.tensor.matmul(out, ll, rh, start=False, stop=stop)

        block = ctx.enter_context(nc.Block())

        @block.sync
        def _(sp):
            sp.dma_start(raw[:, 0, :, :], chunk_rows(dst[0:EP])).then_inc(raw_loaded, 16)
            sp.dma_start(raw[:, 1, :, :], chunk_rows(dst[1:EP + 1])).then_inc(raw_loaded, 16)
            sp.dma_start(raw[:, 2, :, :], chunk_rows(src)).then_inc(raw_loaded, 16)
            sp.dma_start(wc[:, :, :, :], w_conv).then_inc(loaded, 16)
            sp.dma_start(we[:, :, :, :], w_edge).then_inc(loaded, 16)
            sp.dma_start(w1[:, :, :], l1_w).then_inc(loaded, 16)
            sp.dma_start(m1[:, :, :], l1_m).then_inc(loaded, 16)
            for to, of in ((bc, b_conv), (be, b_edge), (gam, gamma), (bet, beta)):
                sp.dma_start(to[:, :, :], of).then_inc(loaded, 16)

            sp.wait_ge(order_known, 1)
            unsorted = sp.value_load(unsorted_i[0:1, 0:1], min_val=0, max_val=1)

            def sort_edges():
                quarter = CHUNKS // 4
                for i in range(4):
                    sp.dma_start(node_i[:, i * quarter:(i + 1) * quarter].unsqueeze(2),
                                 dst[i * quarter * P:(i + 1) * quarter * P].rearrange("(c p) -> p c", p=P).unsqueeze(2),
                                 allow_slow_non_contiguous=True).then_inc(
                        columns_loaded, 16)
                for b in range(BLOCKS):
                    wait(sp, block_used, b)
                    sp.dma_start(block_i, dst[b * BLOCK:(b + 1) * BLOCK].unsqueeze(0).to_broadcast(
                        [P, BLOCK])).then_inc(block_loaded, 16)
                sp.dma_start(dst_sorted[EP:EP + 1, :], dst[EP:EP + 1].unsqueeze(1)).then_inc(end_stored, 16)

                def load_chunk(c):
                    if isinstance(c, int):
                        sp.wait_ge(ranks_made, 1)
                    else:
                        wait_alone(sp, chunk_scattered, 48 * c, sp_passed)
                    at = bass.ds(c * P, P)
                    sp.dma_start(dst_stage[:, :], dst[at].unsqueeze(1)).then_inc(chunk_loaded, 16)
                    sp.dma_start(src_stage[:, :], src[at].unsqueeze(1)).then_inc(chunk_loaded, 16)
                    sp.dma_start(got[:, 0, 0, :], edge[at, :]).then_inc(chunk_loaded, 16)

                load_chunk(0)
                with sp.Fori(1, CHUNKS) as c:
                    load_chunk(c)
                sp.wait_ge(chunk_scattered, 48 * CHUNKS)
                sp.wait_ge(end_stored, 16)
                for i, of in enumerate((dst_sorted[0:EP, 0], dst_sorted[1:EP + 1, 0], src_sorted[:, 0])):
                    sp.dma_start(raw[:, i, :, :], chunk_rows(of)).then_inc(raw_reloaded, 16)

            with sp.If(unsorted != 0):
                sort_edges()
            sp.wait_ge(const_made, 4)
            sp.dma_start(row_of_v, zero_rows[:, :]).then_inc(tables_stored, 16)
            sp.dma_start(sums[ZERO:ZERO + P, :], res[:, 0, 0, :]).then_inc(tables_stored, 16)
            sp.wait_ge(tables_stored, 32)

            def destinations_load(k, q, of):
                g, p, i = number(k, q)
                wait_alone(sp, same_made, g - 1, sp_passed)
                sp.dma_start(drow[:, p, :], of.rearrange("(g j) -> g j", j=QUAD * P)[bass.ds(g, 1), :].to_broadcast([P, QUAD * P])).then_inc(
                    drow_loaded[p], 16)

            def sparse_load(s, k, q, edges=edge_v):
                g, p, i = number(k, q)
                u, v = NS[p] * s + i, NS4[q] * s + k
                if s == 0:
                    if not starts(k, q, SLOTS):
                        wait_alone(sp, e_turned, g - SLOTS + 1, sp_passed)
                        wait_alone(sp, msg_summed, g - SLOTS + 1, sp_passed)
                    sp.dma_start(ein[:, q, :].rearrange("p (c f) -> p c f", f=D),
                                 edges[:, bass.ds(g * QUAD, QUAD), :]).then_inc(e_loaded[q], 16)
                elif s < FINAL:
                    wait_alone(sp, e_shifted, EGROUPS * (s - 1) + g - SLOTS + 1, sp_passed)
                    if s <= LAYERS - 1:
                        wait_alone(sp, e_product, H * (EGROUPS * s + g - SLOTS + 1), sp_passed)
                    sp.dma_start(ein[:, q, :],
                                 edge_t[bass.ds(g, 1), :, :].rearrange("o p f -> (o p) f")).then_inc(e_loaded[q], 16)

            def sparse_store(s, k, q):
                g, p, i = number(k, q)
                wait_alone(sp, sums_out, EGROUPS * s + g + 1, sp_passed)
                sp.dma_start(sums_v[:, bass.ds(g * QUAD, QUAD), :], res[:, p, :, :]).then_inc(sums_stored[p], 16)
                if s < LAYERS:
                    wait_alone(sp, e_updated, H * (EGROUPS * s + g + 1), sp_passed)
                    sp.dma_start(edge_t[bass.ds(g, 1), :, :].rearrange("o p f -> (o p) f"),
                                 tout[:, p, :, :].rearrange("p h j -> p (h j)")).then_inc(e_stored[p], 16)

            def dense_load(d, k, q):
                g, p, i = number(k, q)
                wait_alone(sp, rows_turned, NGROUPS * d + g - SLOTS + 1, sp_passed)
                if d == FINAL:
                    wait_alone(sp, ln, ln_read(d, k, q, SLOTS), sp_passed)
                table = x_v if d == 0 else nodes_v
                sp.dma_start(rows[:, q, :, :], table[:, bass.ds(g * QUAD, QUAD), :]).then_inc(rows_loaded[q], 16)

            def input_load(k, q):
                g, p, i = number(k, q)
                wait_alone(sp, ln, ln_read(LAST, k, q, 2), sp_passed)
                sp.dma_start(ein[:, p, :].rearrange("p (t f) -> p t f", f=D),
                             x_v[:, bass.ds(g * QUAD, QUAD), :]).then_inc(x_loaded[p], 16)

            def dense_store(d, k, q):
                g, p, i = number(k, q)
                if d < LAST:
                    wait_alone(sp, rows_out, NGROUPS * d + g + 1, sp_passed)
                else:
                    wait_alone(sp, ln_out, NGROUPS * (d - LAST) + g + 1, sp_passed)
                table = out_v if d == FINAL else nodes_v
                sp.dma_start(table[:, bass.ds(g * QUAD, QUAD), :], res[:, p, :, :]).then_inc(nodes_stored[p], 16)

            for s in range(SPARSE):
                if s > 0:
                    if s <= LAYERS:
                        for p in range(2):
                            sp.wait_ge(e_stored[p], 16 * NS[p] * s)
                def sparse_traffic(edges, destinations):
                    for g in range(2 if s == 0 else 0):
                        destinations_load(*place(g), destinations)
                    for g in range(SLOTS - 1):
                        sparse_load(s, *place(g), edges)

                    def sparse_step(k, q):
                        if s == 0:
                            destinations_load(*ahead(k, q, 2), destinations)
                        sparse_load(s, *ahead(k, q, SLOTS - 1), edges)
                        if not starts(k, q, 1):
                            sparse_store(s, *behind(k, q))

                    over_groups(sp, 0, EGROUPS - SLOTS + 1, sparse_step)
                    if s == 0:
                        destinations_load(*place(EGROUPS - 1), destinations)

                if s == 0:
                    with sp.If(unsorted != 0):
                        sparse_traffic(edge_sorted_v, dst_sorted[0:EP, 0])
                    with sp.Else():
                        sparse_traffic(edge_v, dst[0:EP])
                else:
                    sparse_traffic(None, None)
                for g in range(EGROUPS - SLOTS, EGROUPS):
                    sparse_store(s, *place(g))
                for p in range(2):
                    sp.wait_ge(sums_stored[p], 16 * NS[p] * (s + 1))
                edges = sums[0:EP, :].rearrange("(h q p) f -> q h p f", h=2, q=CH)
                sp.dma_start(run_last[:, :, :], edges[:, :, P - 1, :]).then_inc(runs_loaded, 16)
                sp.dma_start(run_first[:, :, :], edges[:, :, 0, :]).then_inc(runs_loaded, 16)
                if s > 0:
                    for p in range(2):
                        sp.wait_ge(nodes_stored[p], 16 * ND * s)
                else:
                    for p in range(2):
                        sp.wait_ge(rows_scattered[p], 16 * QUAD * NS[p])
                    sp.dma_start(row_idx[:, :], row_of_v).then_inc(row_idx_loaded, 16)
                for g in range(SLOTS - 1):
                    dense_load(s, *place(g))
                sp.wait_ge(runs_summed, s + 1)
                sp.dma_start(sums[SPAN:SPAN + CHUNKS, :].rearrange("(h q) f -> q h f", h=2),
                             run_sum[:, :, :]).then_inc(runs_stored, 16)

                def dense_step(loads):
                    def run(k, q):
                        if loads:
                            dense_load(s, *ahead(k, q, SLOTS - 1))
                        if s == LAST:
                            input_load(k, q)
                        if not starts(k, q, 2):
                            dense_store(s, *behind(k, q, 2))
                    return run

                over_groups(sp, 0, NGROUPS - SLOTS + 1, dense_step(True))
                over_groups(sp, NGROUPS - SLOTS + 1, NGROUPS, dense_step(False))
                for g in range(NGROUPS - 2, NGROUPS):
                    dense_store(s, *place(g))
                for p in range(2):
                    sp.wait_ge(nodes_stored[p], 16 * ND * (s + 1))

        @block.gpsimd
        def _(pool):
            nc.gpsimd.memset(ones[:, :], 1.0).then_inc(const_made, 1)
            nc.gpsimd.memset(res[:, 0, :, :], 0.0).then_inc(const_made, 1)
            nc.gpsimd.iota(zero_rows[:, :], pattern=[[0, TILES]], base=ZERO, channel_multiplier=1).then_inc(const_made, 1)
            nc.gpsimd.iota(j_i[:, :], pattern=[[P, CHUNKS]], base=0, channel_multiplier=1).then_inc(const_made, 1)
            nc.gpsimd.iota(span_i[:, :], pattern=[[1, CHUNKS]], base=SPAN, channel_multiplier=0).then_inc(const_made, 1)
            pool.wait_ge(const_made, 5)
            nc.gpsimd.affine_select(out=ident[:, :], in_=ones[:, :], compare_op=ALU.is_equal, fill=0.0, base=0,
                                    pattern=[[-1, P]], channel_multiplier=1).then_inc(const_made, 1)
            nc.gpsimd.affine_select(out=sel_last[:, :], in_=ones[:, :], compare_op=ALU.is_equal, fill=0.0,
                                    base=-(P - 1), pattern=[[0, P]], channel_multiplier=1).then_inc(const_made, 1)
            nc.gpsimd.affine_select(out=sel_first[:, :], in_=ones[:, :], compare_op=ALU.is_equal, fill=0.0,
                                    base=0, pattern=[[0, P]], channel_multiplier=1).then_inc(const_made, 1)
            pool.wait_ge(order_known, 1)
            unsorted = pool.value_load(unsorted_i[0:1, 0:1], min_val=0, max_val=1)

            def scatter_chunk(c):
                if not isinstance(c, int):
                    wait_alone(pool, chunk_scattered, 48 * c, pool_passed)
                nc.gpsimd.tensor_copy(rank_stage[:, :], row_i[:, bass.ds(c, 1)]).then_inc(rank_staged, 1)
                wait_alone(pool, rank_staged, c + 1, pool_passed)
                wait_alone(pool, chunk_loaded, 48 * c + 48, pool_passed)
                for to, of in ((dst_sorted, dst_stage[:, :]), (src_sorted, src_stage[:, :]),
                               (edge_sorted, got[:, 0, 0, :])):
                    nc.gpsimd.indirect_dma_start(
                        out=to, out_offset=bass.IndirectOffsetOnAxis(ap=rank_stage[:, 0:1], axis=0),
                        in_=of, in_offset=None).then_inc(chunk_scattered, 16)

            with pool.If(unsorted != 0):
                nc.gpsimd.iota(place_i, pattern=[[1, BLOCK]], base=0, channel_multiplier=0).then_inc(places_made, 1)
                pool.wait_ge(ranks_made, 1)
                scatter_chunk(0)
                with pool.Fori(1, CHUNKS) as c:
                    scatter_chunk(c)
                pool.wait_ge(chunk_scattered, 48 * CHUNKS)
            pool.wait_ge(prep, 10)
            for h in range(2):
                nc.gpsimd.affine_select(out=links[:, h, :], in_=links[:, h, :], compare_op=ALU.is_gt, fill=0.0,
                                        base=-CH * h, pattern=[[1, CHUNKS]], channel_multiplier=-1).then_inc(links_made, 1)

            def gather(table, index, to, done):
                nc.gpsimd.indirect_dma_start(
                    out=to, out_offset=None, in_=table,
                    in_offset=bass.IndirectOffsetOnAxis(ap=index, axis=0)).then_inc(done, 16)

            for s in range(SPARSE):
                def stage_scatter(k, q):
                    g, p, i = number(k, q)
                    wait_alone(pool, rows_scattered[p], 16 * QUAD * i, pool_passed)
                    at = bass.ds(g * QUAD, QUAD)
                    nc.gpsimd.tensor_copy(row_stage[:, p, :], row_i[:, at]).then_inc(stage_copied, 1)
                    nc.gpsimd.tensor_copy(node_stage[:, p, :], node_i[:, at]).then_inc(stage_copied, 1)

                def scatter(k, q):
                    g, p, i = number(k, q)
                    wait_alone(pool, stage_copied, 2 * (g + 1), pool_passed)
                    for c in range(QUAD):
                        nc.gpsimd.indirect_dma_start(
                            out=row_of, out_offset=bass.IndirectOffsetOnAxis(ap=node_stage[:, p, c:c + 1], axis=0),
                            in_=row_stage[:, p, c:c + 1], in_offset=None, bounds_check=NP - 1,
                            oob_is_err=False).then_inc(rows_scattered[p], 16)

                def sparse_step(k, q):
                    if s == 0 and not starts(k, q, 2):
                        stage_scatter(*behind(k, q, 2))
                    sparse_gather(k, q)
                    if s == 0 and not starts(k, q, 2):
                        scatter(*behind(k, q, 2))

                def sparse_gather(k, q):
                    g, p, i = number(k, q)
                    u, v = NS[p] * s + i, NS4[q] * s + k
                    wait_alone(pool, sp_got[q], 16 * QUAD * v, pool_passed)
                    nc.gpsimd.tensor_copy(idx[:, q, :], src_i[:, bass.ds(g * QUAD, QUAD)]).then_inc(idx_staged, 1)
                    wait_alone(pool, idx_staged, (EGROUPS + NGROUPS) * s + g + 1, pool_passed)
                    if s < FINAL:
                        wait_alone(pool, msg_made, EGROUPS * s + g - SLOTS + 1, pool_passed)
                    else:
                        wait_alone(pool, seg_turned, g - SLOTS + 1, pool_passed)
                    for c in range(QUAD):
                        gather(x if s == 0 else nodes, idx[:, q, c:c + 1], got[:, q, c, :], sp_got[q])

                if s > 0:
                    for p in range(2):
                        pool.wait_ge(nodes_stored[p], 16 * ND * s)
                else:
                    pool.wait_ge(prep, 10)
                    pool.wait_ge(tables_stored, 32)
                over_groups(pool, 0, EGROUPS, sparse_step)
                if s == 0:
                    for g in (EGROUPS - 2, EGROUPS - 1):
                        stage_scatter(*place(g))
                        scatter(*place(g))
                for q in range(SLOTS):
                    pool.wait_ge(sp_got[q], 16 * QUAD * NS4[q] * (s + 1))

                def dense_gather(k, q):
                    g, p, i = number(k, q)
                    u, v = ND * s + i, ND4[q] * s + k
                    wait_alone(pool, dn_got[q], 16 * QUAD * v, pool_passed)
                    nc.gpsimd.tensor_copy(idx[:, q, :], row_idx[:, bass.ds(g * QUAD, QUAD)]).then_inc(idx_staged, 1)
                    wait_alone(pool, idx_staged, (EGROUPS + NGROUPS) * s + EGROUPS + g + 1, pool_passed)
                    if s < FINAL:
                        wait_alone(pool, turned, NGROUPS * s + g - SLOTS + 1, pool_passed)
                    else:
                        wait_alone(pool, ln, ln_read(s, k, q, SLOTS), pool_passed)
                    for t in range(QUAD):
                        gather(sums, idx[:, q, t:t + 1], got[:, q, t, :], dn_got[q])

                pool.wait_ge(row_idx_loaded, 16)
                for p in range(2):
                    pool.wait_ge(sums_stored[p], 16 * NS[p] * (s + 1))
                pool.wait_ge(runs_stored, 16 * (s + 1))
                over_groups(pool, 0, NGROUPS, dense_gather)
                for q in range(SLOTS):
                    pool.wait_ge(dn_got[q], 16 * QUAD * ND4[q] * (s + 1))

        @block.tensor
        def _(pe):
            pe.wait_ge(const_made, 8)
            pe.wait_ge(order, 3)
            nc.tensor.matmul(ps_back[:, 0, 0:1], ones[0:CH, :], bad_any[:, 0:1], start=True, stop=True).then_inc(order_pe, 1)
            pe.wait_ge(prep, 1)
            pe.wait_ge(const_made, 8)
            for i, ps in enumerate((ps_in, ps_agg, ps_out)):
                for h in range(2):
                    last = nc.tensor.transpose(ps[:, 0, h * CH:(h + 1) * CH], rawf[:, i, h, :], ident[0:CH, 0:CH])
            last.then_inc(prep_pe, 1)
            pe.wait_ge(prep, 2)
            nc.tensor.matmul(ps_back[:, 0, 0:CHUNKS], sel_last[:, :], dcol[:, :], start=True, stop=True)
            nc.tensor.matmul(ps_back[:, 1, 0:CHUNKS], sel_first[:, :], dcol[:, :], start=True,
                             stop=True).then_inc(prep_pe, 1)
            pe.wait_ge(loaded, 16 * 8)
            pe.wait_ge(prep, 8)

            def sparse(s):
                def turn_edges(k, q):
                    g, p, i = number(k, q)
                    u, v = NS[p] * s + i, NS4[q] * s + k
                    if s == 0:
                        pe.wait_ge(e_loaded[q], 16 * (v + 1))
                        wait(pe, e_split, H * (g - 1))
                        for h in range(H):
                            for c in range(QUAD):
                                last = nc.tensor.transpose(
                                    ps_edges[p][:, h, c * P:(c + 1) * P],
                                    ein[:, q, c * D + h * P:c * D + (h + 1) * P], ident[:, :])
                    else:
                        pe.wait_ge(e_shifted, EGROUPS * (s - 1) + g + 1)
                        wait(pe, msg_summed, EGROUPS * s + g - 1)
                        for c in range(QUAD):
                            for h in range(H):
                                last = nc.tensor.transpose(as_rows(ps_edges[p])[:, c, h * P:(h + 1) * P],
                                                           tin[:, p, h, c * P:(c + 1) * P], ident[:, :])
                    last.then_inc(e_turned, 1)

                def update_edges(k, q):
                    g, p, i = number(k, q)
                    G = EGROUPS * s + g
                    pe.wait_ge(e_split, H * (G + 1))
                    for ho in range(H):
                        wait(pe, e_updated, H * G - H + 1 + ho)
                        for h in range(H):
                            cols = slice(ho * P, (ho + 1) * P)
                            last = three_products(
                                ps_out[:, ho, :], ((we_high[:, h, cols], we_low[:, h, cols]),
                                                   (tin_high[:, p, h, :], tin_low[:, p, h, :])), h == 0, h == H - 1)
                        last.then_inc(e_product, 1)

                def sum_messages(k, q):
                    g, p, i = number(k, q)
                    pe.wait_ge(same_made, EGROUPS * s + g + 1)
                    pe.wait_ge(msg_made, EGROUPS * s + g + 1)
                    wait(pe, sums_out, EGROUPS * s + g)
                    for c in range(QUAD):
                        last = nc.tensor.matmul(as_rows(ps_agg)[:, c, :], same[:, p, c, :], mid[:, p, c, :],
                                                start=True, stop=True)
                    last.then_inc(sums_made, 1)

                def step(k, q):
                    if not (isinstance(k, int) and SLOTS * k + q == EGROUPS - 1):
                        turn_edges(*ahead(k, q))
                    if s < LAYERS:
                        update_edges(k, q)
                    sum_messages(k, q)

                pe.wait_ge(weights_split, 4 * (s + 1))
                turn_edges(0, 0)
                over_groups(pe, 0, EGROUPS - 1, step)
                step(*place(EGROUPS - 1))

            def sparse_final():
                s = FINAL

                def sum_turned(k, q):
                    g, p, i = number(k, q)
                    u, v = NS[p] * s + i, NS4[q] * s + k
                    pe.wait_ge(sp_got[q], 16 * QUAD * (v + 1))
                    pe.wait_ge(same_made, EGROUPS * s + g + 1)
                    wait(pe, seg_split, H * (g - 1))
                    for c in range(QUAD):
                        for h in range(H):
                            last = nc.tensor.matmul(ps_edges[p][:, h, c * P:(c + 1) * P], got[:, q, c, h * P:(h + 1) * P],
                                                    same[:, p, c, :], start=True, stop=True)
                    last.then_inc(seg_turned, 1)

                def times_m(k, q):
                    g, p, i = number(k, q)
                    pe.wait_ge(seg_split, H * (g + 1))
                    wait(pe, sums_out, EGROUPS * s + g)
                    for c in range(QUAD):
                        for h in range(H):
                            cols = slice(c * P, (c + 1) * P)
                            last = three_products(
                                as_rows(ps_agg)[:, c, :], ((tin_high[:, p, h, cols], tin_low[:, p, h, cols]),
                                                           (we_high[:, h, :], we_low[:, h, :])), h == 0, h == H - 1)
                    last.then_inc(sums_made, 1)

                def step(k, q):
                    sum_turned(k, q)
                    times_m(*behind(k, q))

                sum_turned(0, 0)
                over_groups(pe, 1, EGROUPS, step)
                times_m(*place(EGROUPS - 1))

            def runs(s):
                pe.wait_ge(runs_loaded, 32 * (s + 1))
                pe.wait_ge(links_made, 2)
                pe.wait_ge(sums_out, EGROUPS * (s + 1))
                for ho in range(2):
                    for h in range(2):
                        last = nc.tensor.matmul(ps_agg[0:CH, ho, 0:D], links[:, h, ho * CH:(ho + 1) * CH],
                                                run_last[:, h, :], start=(h == 0), stop=(h == 1))
                last.then_inc(runs_product, 1)
                pe.wait_ge(runs_summed, s + 1)

            def dense(d):
                def turn_in(k, q):
                    g, p, i = number(k, q)
                    u, v = ND * d + i, ND4[q] * d + k
                    pe.wait_ge(rows_loaded[q], 16 * (v + 1))
                    to = ps_rows[p] if d == FINAL else ps_in
                    wait(pe, scaled, H * (NGROUPS * d + g - (1 if d == FINAL else 0)))
                    for h in range(H):
                        for t in range(QUAD):
                            last = nc.tensor.transpose(to[:, h, t * P:(t + 1) * P],
                                                       rows[:, q, t, h * P:(h + 1) * P], ident[:, :])
                    last.then_inc(rows_turned, 1)
                    if d < FINAL:
                        pe.wait_ge(dn_got[q], 16 * QUAD * (v + 1))
                        wait(pe, added, H * (NGROUPS * d + g))
                        for h in range(H):
                            for t in range(QUAD):
                                last = nc.tensor.transpose(ps_agg[:, h, t * P:(t + 1) * P],
                                                           got[:, q, t, h * P:(h + 1) * P], ident[:, :])
                        last.then_inc(turned, 1)

                def main(k, q):
                    g, p, i = number(k, q)
                    G = NGROUPS * d + g
                    if d < FINAL:
                        pe.wait_ge(z_split, H * (G + 1))
                        for ho in range(H):
                            wait(pe, activated, H * G - H + 1 + ho)
                            for h in range(H):
                                cols = slice(ho * P, (ho + 1) * P)
                                last = three_products(
                                    ps_out[:, ho, :], ((wc_high[:, h, cols], wc_low[:, h, cols]),
                                                       (tin_high[:, p, h, :], tin_low[:, p, h, :])), h == 0, h == H - 1)
                            last.then_inc(product, 1)
                    else:
                        pe.wait_ge(scaled, H * (G + 1))
                        wait(pe, ln, ln_read(d, k, q, 2) - 1)
                        for t in range(QUAD):
                            for h in range(H):
                                last = nc.tensor.matmul(as_rows(ps_final[p])[:, t, :], tin[:, p, h, t * P:(t + 1) * P],
                                                        w1[:, h, :], start=(h == 0), stop=(h == H - 1))
                        last.then_inc(product, 1)

                def turn_back(k, q):
                    g, p, i = number(k, q)
                    pe.wait_ge(activated, H * (NGROUPS * d + g + 1))
                    if d < LAST:
                        wait(pe, rows_out, NGROUPS * d + g)
                    else:
                        wait(pe, ln, ln_read(d, k, q, 1))
                    for t in range(QUAD):
                        for h in range(H):
                            last = nc.tensor.transpose(as_rows(ps_back)[:, t, h * P:(h + 1) * P],
                                                       tout[:, p, h, t * P:(t + 1) * P], ident[:, :])
                    last.then_inc(back, 1)

                def step(k, q):
                    turn_in(*ahead(k, q))
                    main(k, q)
                    if d < FINAL and not starts(k, q, 1):
                        turn_back(*behind(k, q))

                end = NGROUPS - 1
                turn_in(0, 0)
                over_groups(pe, 0, end, step)
                main(*place(end))
                if d < FINAL:
                    turn_back(*place(end - 1))
                    turn_back(*place(end))

            for s in range(SPARSE):
                sparse_final() if s == FINAL else sparse(s)
                runs(s)
                dense(s)
                if s < LAYERS:
                    pe.wait_ge(bn, BN_STEPS * (s + 1))
                    for h in range(H):
                        last = nc.tensor.matmul(ps_back[:, 0, h * P:(h + 1) * P], ones[:, :], diag[:, h, :],
                                                start=True, stop=True)
                    last.then_inc(bn_row, 1)
                    pe.wait_ge(bn_row_out, s + 1)

        @block.scalar
        def _(act):
            def sparse(s):
                def messages(k, q):
                    g, p, i = number(k, q)
                    act.wait_ge(msg_summed, EGROUPS * s + g + 1)
                    wait(act, sums_made, EGROUPS * s + g - 1)
                    nc.scalar.activation(mid[:, p, :, :], got[:, q, :, :], ACT.Relu).then_inc(msg_made, 1)

                def updates(k, q):
                    g, p, i = number(k, q)
                    for ho in range(H):
                        act.wait_ge(e_product, H * (EGROUPS * s + g) + ho + 1)
                        wait(act, e_stored[p], 16 * (NS[p] * s + i))
                        nc.scalar.activation(tout[:, p, ho, :], ps_out[:, ho, :], ACT.Relu,
                                             bias=be[:, s, ho:ho + 1]).then_inc(e_updated, 1)

                def results(k, q):
                    g, p, i = number(k, q)
                    act.wait_ge(sums_made, EGROUPS * s + g + 1)
                    wait(act, sums_stored[p], 16 * (NS[p] * s + i))
                    nc.scalar.copy(res[:, p, :, :], as_rows(ps_agg)).then_inc(sums_out, 1)

                def high_edges(k, q):
                    g, p, i = number(k, q)
                    G, v = EGROUPS * s + g, NS4[q] * s + k
                    for h in range(H):
                        if s == 0:
                            act.wait_ge(e_turned, g + 1)
                            of = ps_edges[p][:, h, :]
                        else:
                            act.wait_ge(e_loaded[q], 16 * (v + 1))
                            of = ein[:, q, h * QUAD * P:(h + 1) * QUAD * P]
                        wait(act, e_product, H * (G - 1))
                        nc.scalar.copy(tin_high[:, p, h, :], of).then_inc(e_high, 1)

                def step(k, q):
                    if s < LAYERS and not (isinstance(k, int) and SLOTS * k + q == EGROUPS - 1):
                        high_edges(*ahead(k, q))
                    messages(k, q)
                    if not starts(k, q, 1):
                        results(*behind(k, q))
                    if s < LAYERS:
                        updates(k, q)

                def turned_sums(k, q):
                    g, p, i = number(k, q)
                    for h in range(H):
                        act.wait_ge(seg_turned, g + 1)
                        wait(act, sums_made, EGROUPS * s + g - 1)
                        nc.scalar.copy(tin_high[:, p, h, :], ps_edges[p][:, h, :]).then_inc(seg_turned_out, 1)

                def final_step(k, q):
                    turned_sums(k, q)
                    results(*behind(k, q))

                if s == FINAL:
                    turned_sums(0, 0)
                    over_groups(act, 1, EGROUPS, final_step)
                else:
                    if s < LAYERS:
                        high_edges(0, 0)
                    over_groups(act, 0, EGROUPS - 1, step)
                    step(*place(EGROUPS - 1))
                results(*place(EGROUPS - 1))

            def dense(d):
                wl = min(d, LAYERS - 1)

                def scale_in(k, q):
                    g, p, i = number(k, q)
                    G = NGROUPS * d + g
                    act.wait_ge(rows_turned, G + 1)
                    for h in range(H):
                        if d == FINAL:
                            wait(act, product, H * NGROUPS * FINAL + g - 1)
                            nc.scalar.copy(tin[:, p, h, :], ps_rows[p][:, h, :]).then_inc(scaled, 1)
                        else:
                            wait(act, product, H * (G - 1))
                            nc.scalar.activation(tin[:, p, h, :], ps_in[:, h, :], ACT.Identity,
                                                 bias=shift[:, h:h + 1], scale=scale[:, h:h + 1]).then_inc(scaled, 1)

                def high_parts(k, q):
                    g, p, i = number(k, q)
                    for h in range(H):
                        act.wait_ge(added, H * (NGROUPS * d + g) + h + 1)
                        nc.scalar.copy(tin_high[:, p, h, :], tin[:, p, h, :]).then_inc(z_high, 1)

                def activate(k, q):
                    g, p, i = number(k, q)
                    G = NGROUPS * d + g
                    for ho in range(H):
                        act.wait_ge(product, H * G + ho + 1)
                        if not starts(k, q, 2):
                            wait(act, back, G - 1)
                            if d < LAYERS:
                                wait(act, counted, H * (G - 1))
                        nc.scalar.activation(tout[:, p, ho, :], ps_out[:, ho, :], ACT.Relu,
                                             bias=bc[:, wl, ho:ho + 1]).then_inc(activated, 1)

                def deviations(k, q):
                    g, p, i = number(k, q)
                    g = NGROUPS * (d - LAST) + g
                    act.wait_ge(ln, LN_STEPS * (g + 1))
                    nc.scalar.activation(ln_std[:, p, :], ln_mv[:, p, :, 1], ACT.Sqrt, bias=eps[:, 0:1]).then_inc(
                        ln_std_made, 1)

                def ln_rows(k, q):
                    g, p, i = number(k, q)
                    g = NGROUPS * (d - LAST) + g
                    act.wait_ge(ln_factored, g + 1)
                    wait(act, nodes_stored[p], 16 * (ND * d + i))
                    for t in range(QUAD):
                        last = nc.scalar.activation(res[:, p, t, :], ln_input(d, q)[:, t, :], ACT.Identity,
                                                    bias=ln_bias[:, p, t:t + 1], scale=ln_rstd[:, p, t:t + 1])
                    last.then_inc(ln_out, 1)

                def step(k, q):
                    scale_in(*ahead(k, q))
                    if d < FINAL:
                        high_parts(*ahead(k, q))
                    if d == LAST and not starts(k, q, 2):
                        deviations(*behind(k, q, 2))
                    if d == FINAL and not starts(k, q, 1):
                        deviations(*behind(k, q))
                    if d < FINAL:
                        activate(k, q)
                    if d >= LAST and not starts(k, q, 2):
                        ln_rows(*behind(k, q, 2))

                end = NGROUPS - 1
                if d == 0:
                    act.wait_ge(prep, 13)
                elif d < FINAL:
                    act.wait_ge(bn, BN_STEPS * min(d, LAYERS))
                scale_in(0, 0)
                if d < FINAL:
                    high_parts(0, 0)
                over_groups(act, 0, end, step)
                if d < FINAL:
                    activate(*place(end))
                if d >= LAST:
                    for g in range(end - 2, end + 1):
                        if d == LAST or g > end - 2:
                            deviations(*place(g))
                        ln_rows(*place(g))

            act.wait_ge(loaded, 16 * 8)
            for s in range(SPARSE):
                if 0 < s < LAYERS:
                    act.wait_ge(back, NGROUPS * s)
                    act.wait_ge(counted, H * NGROUPS * s)
                sparse(s)
                if s < LAYERS:
                    for p in range(2):
                        act.wait_ge(e_stored[p], 16 * NS[p] * (s + 1))
                dense(s)
                if s < LAYERS:
                    act.wait_ge(bn, BN_STEPS * s + 1)
                    nc.scalar.activation(bn_std[:, :], mv[:, :, 1], ACT.Sqrt, bias=eps[:, 0:1]).then_inc(bn_std_made, 1)
                    act.wait_ge(bn_row, s + 1)
                    nc.scalar.copy(scale_row[:, :], ps_back[:, 0, 0:D]).then_inc(bn_row_out, 1)

        @block.vector
        def _(dve):
            dve.wait_ge(raw_loaded, 48)
            nc.vector.tensor_copy(rawf[:, :, :, :], raw[:, :, :, :]).then_inc(order, 1)
            dve.wait_ge(order, 1)
            nc.vector.tensor_tensor(bad[:, :, :], rawf[:, 0, :, :], rawf[:, 1, :, :], ALU.is_gt).then_inc(order, 1)
            dve.wait_ge(order, 2)
            nc.vector.tensor_reduce(bad_any[:, :], bad[:, :, :].rearrange("q h p -> q (h p)"),
                                    mybir.AxisListType.X, ALU.max).then_inc(order, 1)
            dve.wait_ge(order_pe, 1)
            nc.vector.tensor_scalar(unsorted_i[:, :], ps_back[:, 0, 0:1], 0.0, None, ALU.is_gt).then_inc(order_known, 1)
            dve.wait_ge(order_known, 1)
            unsorted = dve.value_load(unsorted_i[0:1, 0:1], min_val=0, max_val=1)

            def rank_edges():
                done = 0

                def then(last):
                    nonlocal done
                    last.then_inc(ranking, 1)
                    done += 1
                    dve.wait_ge(ranking, done)

                dve.wait_ge(columns_loaded, 64)
                then(nc.vector.tensor_copy(dcol[:, :], node_i[:, :]))
                dve.wait_ge(const_made, 8)
                then(nc.vector.tensor_copy(j_f[:, :], j_i[:, :]))
                dve.wait_ge(places_made, 1)
                then(nc.vector.tensor_copy(places, place_i))
                for b in range(BLOCKS):
                    dve.wait_ge(block_loaded, 16 * (b + 1))
                    then(nc.vector.tensor_copy(block_dst, block_i))
                    then(nc.vector.tensor_scalar(span_f[:, :], j_f[:, :], float(-b * BLOCK), None, ALU.add))
                    base = done
                    with dve.Fori(0, CHUNKS) as c:
                        at = bass.ds(c, 1)
                        step = 7 * c + base
                        nc.vector.tensor_copy(column[:, 0:1], dcol[:, at]).then_inc(ranking, 1)
                        nc.vector.tensor_copy(column[:, 1:2], span_f[:, at]).then_inc(ranking, 1)
                        wait_alone(dve, ranking, step + 2, dve_passed)
                        nc.vector.tensor_scalar(block_earlier, places, column[:, 1:2], None, ALU.is_lt).then_inc(ranking, 1)
                        wait_alone(dve, ranking, step + 3, dve_passed)
                        nc.vector.scalar_tensor_tensor(out=block_earlier, in0=block_dst, scalar=column[:, 0:1],
                                                       in1=block_earlier, op0=ALU.is_equal, op1=ALU.mult).then_inc(ranking, 1)
                        wait_alone(dve, ranking, step + 4, dve_passed)
                        nc.vector.scalar_tensor_tensor(out=block_less, in0=block_dst, scalar=column[:, 0:1],
                                                       in1=block_earlier, op0=ALU.is_lt, op1=ALU.add).then_inc(ranking, 1)
                        wait_alone(dve, ranking, step + 5, dve_passed)
                        nc.vector.tensor_reduce(before_count[:, :], block_less, mybir.AxisListType.X,
                                                ALU.add).then_inc(ranking, 1)
                        wait_alone(dve, ranking, step + 6, dve_passed)
                        nc.vector.tensor_copy(counts[:, b, at], before_count[:, :]).then_inc(ranking, 1)
                    done += 7 * CHUNKS
                    dve.wait_ge(ranking, done)
                    nc.vector.memset(tmp[:, :], 0.0).then_inc(block_used, 1)
                for b in range(1, BLOCKS):
                    then(nc.vector.tensor_tensor(counts[:, 0, :], counts[:, 0, :], counts[:, b, :], ALU.add))
                nc.vector.tensor_copy(row_i[:, :], counts[:, 0, :]).then_inc(ranks_made, 1)
                dve.wait_ge(ranks_made, 1)
                dve.wait_ge(raw_reloaded, 48)

            with dve.If(unsorted != 0):
                rank_edges()
            nc.vector.tensor_copy(rawf[:, :, :, :], raw[:, :, :, :]).then_inc(prep, 1)
            dve.wait_ge(prep_pe, 1)
            nc.vector.tensor_copy(dcol[:, :], ps_in[:, 0, 0:CHUNKS]).then_inc(prep, 1)
            nc.vector.tensor_copy(src_i[:, :], ps_out[:, 0, 0:CHUNKS]).then_inc(prep, 1)
            nc.vector.tensor_copy(dnext[:, :], ps_agg[:, 0, 0:CHUNKS]).then_inc(prep, 1)
            nc.vector.memset(prev_last[:, 0:1], -1.0).then_inc(prep, 1)
            dve.wait_ge(prep_pe, 2)
            nc.vector.tensor_copy(prev_last[:, 1:CHUNKS], ps_back[:, 0, 0:CHUNKS - 1]).then_inc(prep, 1)
            nc.vector.tensor_copy(first_row[:, :], ps_back[0:CH, 1, 0:CHUNKS]).then_inc(prep, 1)
            dve.wait_ge(const_made, 8)
            nc.vector.tensor_copy(j_f[:, :], j_i[:, :]).then_inc(prep, 1)
            dve.wait_ge(prep, 8)
            nc.vector.tensor_tensor(flag[:, :], prev_last[:, :], dcol[:, :], ALU.is_equal).then_inc(steps, 1)
            nc.vector.tensor_tensor(span_f[:, :], span_i[:, :], j_f[:, :], ALU.subtract).then_inc(steps, 1)
            dve.wait_ge(steps, 2)
            nc.vector.tensor_tensor(span_f[:, :], span_f[:, :], flag[:, :], ALU.mult).then_inc(steps, 1)
            dve.wait_ge(steps, 3)
            nc.vector.tensor_tensor(row_i[:, :], span_f[:, :], j_f[:, :], ALU.add).then_inc(steps, 1)
            nc.vector.tensor_tensor(flag[:, :], dnext[:, :], dcol[:, :], ALU.is_equal).then_inc(steps, 1)
            dve.wait_ge(steps, 5)
            nc.vector.scalar_tensor_tensor(out=node_i[:, :], in0=flag[:, :], scalar=float(PAD_DST), in1=dcol[:, :],
                                           op0=ALU.mult, op1=ALU.add).then_inc(steps, 1)
            nc.vector.tensor_scalar(links[:, 0, :], first_row[:, :], rawf[:, 0, 0, P - 1:P], None, ALU.is_equal).then_inc(steps, 1)
            nc.vector.tensor_scalar(links[:, 1, :], first_row[:, :], rawf[:, 0, 1, P - 1:P], None, ALU.is_equal).then_inc(steps, 1)
            dve.wait_ge(steps, 8)
            nc.vector.memset(tmp[:, :], 0.0).then_inc(prep, 1)
            nc.vector.memset(mv[:, :, :], 0.0).then_inc(prep, 1)
            nc.vector.memset(scale[:, :], 1.0).then_inc(prep, 1)
            nc.vector.memset(shift[:, :], 0.0).then_inc(prep, 1)
            nc.vector.memset(eps[:, :], EPS).then_inc(prep, 1)
            dve.wait_ge(loaded, 16 * 8)
            dve.wait_ge(prep, 13)

            def sparse(s):
                def find_same(k, q):
                    g, p, i = number(k, q)
                    u, v = NS[p] * s + i, NS4[q] * s + k
                    if s < FINAL:
                        wait(dve, sums_made, EGROUPS * s + g - 1)
                    else:
                        wait(dve, seg_turned, g - 1)
                    kept = same_all[:, bass.ds(g * QUAD, QUAD), :]
                    if s > 0:
                        nc.vector.tensor_copy(same[:, p, :, :], kept).then_inc(same_made, 1)
                        return
                    dve.wait_ge(drow_loaded[p], 16 * (u + 1))
                    nc.vector.tensor_tensor(
                        same[:, p, :, :], drow[:, p, :].rearrange("p (c j) -> p c j", c=QUAD),
                        dcol[:, bass.ds(g * QUAD, QUAD)].unsqueeze(2).to_broadcast([P, QUAD, P]),
                        ALU.is_equal).then_inc(same_made, 1)
                    dve.wait_ge(same_made, g + 1)
                    nc.vector.tensor_copy(kept, same[:, p, :, :]).then_inc(same_kept, 1)

                def shift_edges(k, q):
                    g, p, i = number(k, q)
                    u, v = NS[p] * s + i, NS4[q] * s + k
                    dve.wait_ge(e_loaded[q], 16 * (v + 1))
                    wait(dve, e_turned, EGROUPS * s + g - 1)
                    for h in range(H):
                        last = nc.vector.tensor_scalar(tin[:, p, h, :], ein[:, q, h * QUAD * P:(h + 1) * QUAD * P],
                                                       shift[:, h:h + 1], None, ALU.add)
                    last.then_inc(e_shifted, 1)

                def messages(k, q):
                    g, p, i = number(k, q)
                    u, v = NS[p] * s + i, NS4[q] * s + k
                    G = EGROUPS * s + g
                    dve.wait_ge(sp_got[q], 16 * QUAD * (v + 1))
                    if s == 0:
                        dve.wait_ge(e_loaded[q], 16 * (v + 1))
                        nc.vector.tensor_tensor(got[:, q, :, :], got[:, q, :, :],
                                                ein[:, q, :].rearrange("p (c f) -> p c f", f=D),
                                                ALU.add).then_inc(msg_summed, 1)
                        return
                    nc.vector.tensor_tensor(got[:, q, :, :], got[:, q, :, :],
                                            scale_row[:, :].unsqueeze(1).to_broadcast([P, QUAD, D]),
                                            ALU.mult).then_inc(got_scaled, 1)
                    dve.wait_ge(got_scaled, G - EGROUPS + 1)
                    dve.wait_ge(e_turned, G + 1)
                    nc.vector.tensor_tensor(got[:, q, :, :], as_rows(ps_edges[p]), got[:, q, :, :],
                                            ALU.add).then_inc(msg_summed, 1)

                def low_edges(k, q):
                    g, p, i = number(k, q)
                    for h in range(H):
                        dve.wait_ge(e_high, H * (EGROUPS * s + g) + h + 1)
                        if s == 0:
                            of = ps_edges[p][:, h, :]
                        else:
                            of = ein[:, q, h * QUAD * P:(h + 1) * QUAD * P]
                        nc.vector.tensor_tensor(tin_low[:, p, h, :], of, tin_high[:, p, h, :].bitcast(F32),
                                                ALU.subtract).then_inc(e_split, 1)

                def low_sums(k, q):
                    g, p, i = number(k, q)
                    for h in range(H):
                        dve.wait_ge(seg_turned_out, H * g + h + 1)
                        nc.vector.tensor_tensor(tin_low[:, p, h, :], ps_edges[p][:, h, :],
                                                tin_high[:, p, h, :].bitcast(F32), ALU.subtract).then_inc(seg_split, 1)

                def step(k, q):
                    if s == FINAL:
                        low_sums(k, q)
                    if s == 0:
                        low_edges(*ahead(k, q))
                    if s < FINAL:
                        messages(k, q)
                    if 0 < s < LAYERS:
                        low_edges(*ahead(k, q))
                    if 0 < s < FINAL and not (isinstance(k, int) and SLOTS * k + q == EGROUPS - 2):
                        shift_edges(*ahead(k, q, 2))
                    find_same(*ahead(k, q))

                if s < FINAL:
                    weights = ((we_high, we_low, we[:, s, :, :] if s < LAYERS else m1[:, :, :]),
                               (wc_high, wc_low, wc[:, min(s, LAYERS - 1), :, :]))
                    for high, _, of in weights:
                        nc.vector.tensor_copy(high[:, :, :], of).then_inc(weights_split, 1)
                    dve.wait_ge(weights_split, 4 * s + 2)
                    for high, rest, of in weights:
                        nc.vector.tensor_tensor(rest[:, :, :], of, high[:, :, :].bitcast(F32),
                                                ALU.subtract).then_inc(weights_split, 1)
                if s > 0:
                    dve.wait_ge(same_kept, EGROUPS)
                if 0 < s < FINAL:
                    dve.wait_ge(bn_row_out, s if s < LAYERS else LAYERS)
                    for g in range(2):
                        shift_edges(*place(g))
                if s < LAYERS:
                    low_edges(0, 0)
                find_same(0, 0)
                end = EGROUPS - 1
                over_groups(dve, 0, end - 1, step)
                step(*place(end - 1))
                (messages if s < FINAL else low_sums)(*place(end))

            def runs(s):
                dve.wait_ge(runs_product, s + 1)
                dve.wait_ge(runs_loaded, 32 * (s + 1))
                if s > 0:
                    dve.wait_ge(runs_stored, 16 * s)
                nc.vector.tensor_tensor(run_sum[:, :, :], ps_agg[0:CH, :, 0:D], run_first[:, :, :],
                                        ALU.add).then_inc(runs_summed, 1)

            def ln_variance(d, k, q, of):
                p = q % 2
                done = ln_read(d, k, q)
                dve.wait_ge(ln, done)
                for t in range(QUAD):
                    last = nc.vector.bn_stats(ln_stats[:, p, t, :], of[:, t, :])
                last.then_inc(ln, 1)
                wait_alone(dve, ln, done + 1, dve_passed)
                for t in range(QUAD):
                    last = nc.vector.bn_aggr(ln_mv[:, p, t, :], ln_stats[:, p, t, :])
                last.then_inc(ln, 1)

            def ln_reciprocal(d, k, q):
                g, p, i = number(k, q)
                g = NGROUPS * (d - LAST) + g
                dve.wait_ge(ln_std_made, g + 1)
                wait(dve, ln_out, g - 1)
                nc.vector.reciprocal(ln_rstd[:, p, :], ln_std[:, p, :]).then_inc(ln_rstd_made, 1)

            def ln_offset(d, k, q):
                g, p, i = number(k, q)
                dve.wait_ge(ln_rstd_made, NGROUPS * (d - LAST) + g + 1)
                nc.vector.scalar_tensor_tensor(out=ln_bias[:, p, :], in0=ln_mv[:, p, :, 0], scalar=-1.0,
                                               in1=ln_rstd[:, p, :], op0=ALU.mult, op1=ALU.mult).then_inc(ln_factored, 1)

            def ln_factors(d, k, q):
                ln_reciprocal(d, k, q)
                ln_offset(d, k, q)

            def dense(d):
                def add_sums(k, q):
                    g, p, i = number(k, q)
                    G = NGROUPS * d + g
                    for h in range(H):
                        dve.wait_ge(turned, G + 1)
                        dve.wait_ge(scaled, H * G + h + 1)
                        nc.vector.tensor_tensor(tin[:, p, h, :], ps_agg[:, h, :], tin[:, p, h, :],
                                                ALU.add).then_inc(added, 1)
                    for h in range(H):
                        dve.wait_ge(z_high, H * G + h + 1)
                        nc.vector.tensor_tensor(tin_low[:, p, h, :], tin[:, p, h, :],
                                                tin_high[:, p, h, :].bitcast(F32), ALU.subtract).then_inc(z_split, 1)

                def count(k, q, full):
                    g, p, i = number(k, q)
                    G = NGROUPS * d + g
                    for h in range(H):
                        dve.wait_ge(activated, H * G + h + 1)
                        to = stats[:, h, bass.ds(g, 1), :].rearrange("p o s -> p (o s)")
                        if full:
                            of = tout[:, p, h, :]
                        else:
                            of = tout[:, p, h, :].rearrange("p (t j) -> p t j", j=P)[:, :, 0:P - 1]
                        nc.vector.bn_stats(to, of).then_inc(counted, 1)

                def copy_rows(k, q):
                    g, p, i = number(k, q)
                    u, v = ND * d + i, ND4[q] * d + k
                    dve.wait_ge(back, NGROUPS * d + g + 1)
                    wait(dve, nodes_stored[p], 16 * u)
                    nc.vector.tensor_copy(res[:, p, :, :], as_rows(ps_back)).then_inc(rows_out, 1)

                def last_conv_rows(k, q):
                    g, p, i = number(k, q)
                    wait(dve, ln_out, g - 1)
                    dve.wait_ge(x_loaded[p], 16 * (i + 1))
                    dve.wait_ge(back, NGROUPS * d + g + 1)
                    nc.vector.scalar_tensor_tensor(
                        out=mid[:, p, :, :], in0=ein[:, p, :].rearrange("p (t f) -> p t f", f=D), scalar=2.0,
                        in1=as_rows(ps_back), op0=ALU.mult, op1=ALU.add).then_inc(ln, 2)
                    ln_variance(d, k, q, mid[:, p, :, :])

                def final_rows(k, q):
                    g, p, i = number(k, q)
                    u, v = ND * d + i, ND4[q] * d + k
                    to = ln_input(d, q)
                    wait(dve, ln_out, NGROUPS * (d - LAST) + g - SLOTS + 1)
                    dve.wait_ge(dn_got[q], 16 * QUAD * (v + 1))
                    dve.wait_ge(product, H * NGROUPS * FINAL + g + 1)
                    nc.vector.tensor_tensor(to, as_rows(ps_final[p]), got[:, q, :, :], ALU.add).then_inc(ln, 1)
                    if not starts(k, q, 1):
                        ln_reciprocal(d, *behind(k, q))
                    dve.wait_ge(ln, ln_read(d, k, q) - 1)
                    nc.vector.scalar_tensor_tensor(out=to, in0=to, scalar=0.0, in1=rows[:, q, :, :],
                                                   op0=ALU.max, op1=ALU.add).then_inc(ln, 1)
                    if not starts(k, q, 1):
                        ln_offset(d, *behind(k, q))
                    ln_variance(d, k, q, to)

                def step(full):
                    def run(k, q):
                        add_sums(*ahead(k, q))
                        if d < LAYERS:
                            count(k, q, full)
                        if d == LAST and not starts(k, q, 2):
                            ln_factors(d, *behind(k, q, 2))
                        if not starts(k, q, 1):
                            (copy_rows if d < LAST else last_conv_rows)(*behind(k, q))
                    return run

                end = NGROUPS - 1
                if d == FINAL:
                    over_groups(dve, 0, NGROUPS, final_rows)
                    ln_factors(d, *place(end))
                    return
                add_sums(0, 0)
                over_groups(dve, 0, FULL, step(True))
                over_groups(dve, FULL, end, step(False))
                if d < LAYERS:
                    count(*place(end), False)
                for g in (end - 1, end):
                    if d == LAST:
                        ln_factors(d, *place(g - 1))
                    (copy_rows if d < LAST else last_conv_rows)(*place(g))
                if d == LAST:
                    ln_factors(d, *place(end))

            def batch_norm(d):
                done = BN_STEPS * d
                dve.wait_ge(counted, H * NGROUPS * (d + 1))
                for h in range(H):
                    last = nc.vector.bn_aggr(mv[:, h, :], stats[:, h, :, :].rearrange("p g s -> p (g s)"))
                last.then_inc(bn, 1)
                dve.wait_ge(bn, done + 1)
                dve.wait_ge(bn_std_made, d + 1)
                nc.vector.reciprocal(rstd[:, :], bn_std[:, :]).then_inc(bn, 1)
                dve.wait_ge(bn, done + 2)
                nc.vector.tensor_tensor(scale[:, :], rstd[:, :], gam[:, d, :], ALU.mult).then_inc(bn, 1)
                dve.wait_ge(bn, done + 3)
                nc.vector.tensor_tensor(tmp[:, :], mv[:, :, 0], scale[:, :], ALU.mult).then_inc(bn, 1)
                for h in range(H):
                    last = nc.vector.tensor_scalar(diag[:, h, :], ident[:, :], scale[:, h:h + 1], None, ALU.mult)
                last.then_inc(bn, 1)
                dve.wait_ge(bn, done + 5)
                nc.vector.tensor_tensor(shift[:, :], bet[:, d, :], tmp[:, :], ALU.subtract).then_inc(bn, 1)
                dve.wait_ge(bn, done + 6)

            for s in range(SPARSE):
                sparse(s)
                runs(s)
                dense(s)
                if s < LAYERS:
                    batch_norm(s)


def kernel(x, src, dst, edge_attr_256, L0_gnn_W_conv, L0_gnn_b_conv, L0_gnn_W_edge, L0_gnn_b_edge, L0_gnn_gamma,
           L0_gnn_beta, L1_gnn_W, L1_gnn_M):
    import numpy as np
    import concourse.bacc as bacc
    from concourse.bass_utils import run_bass_kernel_spmd

    def pad(a, rows, value=0):
        a = np.asarray(a)
        return np.concatenate([a, np.full((rows - a.shape[0],) + a.shape[1:], value, a.dtype)])

    def halves(w):
        w = np.asarray(w)
        lead = w.shape[:-2]
        w = w.reshape(lead + (H, P, w.shape[-1]))
        return np.ascontiguousarray(np.moveaxis(w, -2, 0))

    def columns(b):
        b = np.asarray(b)
        return np.ascontiguousarray(np.moveaxis(b.reshape(b.shape[0], H, P), -1, 0))

    dst_padded = pad(pad(dst, EP, PAD_DST), EP + 1, END_DST)
    arrays = {
        "x": pad(x, NP), "src": pad(src, EP), "dst": dst_padded, "edge": pad(edge_attr_256, EP),
        "w_conv": halves(L0_gnn_W_conv), "b_conv": columns(L0_gnn_b_conv), "w_edge": halves(L0_gnn_W_edge),
        "b_edge": columns(L0_gnn_b_edge), "gamma": columns(L0_gnn_gamma), "beta": columns(L0_gnn_beta),
        "l1_w": halves(L1_gnn_W), "l1_m": halves(L1_gnn_M),
    }
    nc = bacc.Bacc("TRN2", target_bir_lowering=False, num_devices=1)
    feeds, args = {}, {}
    for name, a in arrays.items():
        feeds[f"in_{name}"] = a
        args[name] = nc.dram_tensor(f"in_{name}", a.shape, mybir.dt.from_np(a.dtype), kind="ExternalInput").ap()
    out = nc.dram_tensor("out_nodes", (NP, D), F32, kind="ExternalOutput").ap()
    gnn_kernel(nc, **args, out=out)
    got = run_bass_kernel_spmd(nc, [feeds], core_ids=[0])
    return got.results[0]["out_nodes"][0:N]
```
